# Optimizing a Trainium2 kernel written in Bass

```python
import numpy as np
import jax
import jax.numpy as jnp

def _softmax(x, axis=-1):
    return jax.nn.softmax(x, axis=axis)

def _gelu(x):
    return jax.nn.gelu(x, approximate=True)

def _silu(x):
    return jax.nn.silu(x)

def _sigmoid(x):
    return jax.nn.sigmoid(x)

def _layernorm(x, axis=-1, eps=1e-05):
    m = jnp.mean(x, axis=axis, keepdims=True)
    v = jnp.var(x, axis=axis, keepdims=True)
    return (x - m) / jnp.sqrt(v + eps)

def _scatter_add(tgt, idx, src, axis=0):
    return tgt.at[idx].add(src)

def _segment_sum(src, seg, n):
    return jax.ops.segment_sum(src, seg, n)
kernel_name = 'mk_sandwich_d1_jaxref_r4_ffcc90'

def setup_inputs(seed: int=0):
    np.random.seed(seed)
    _w = jnp.asarray

    def _L0_attn_setup():
        import jax, jax.numpy as jnp
        import numpy as np
        DIM = 512
        N_HEADS = 32
        N_KV_HEADS = 8
        HEAD_DIM = 64
        REPEATS = N_HEADS // N_KV_HEADS
        SLIDING_WINDOW = 256
        EPS = 1e-06
        B, T = (2, 512)

        def _alibi_slopes(n):
            r = 2.0 ** (-8.0 / n)
            return jnp.asarray([r ** i for i in range(n)], dtype=jnp.float32)

        def _rms_norm(x, w, eps):
            var = jnp.mean(x * x, axis=-1, keepdims=True)
            return x * jax.lax.rsqrt(var + eps) * w
        key = jax.random.key(seed)
        ks = jax.random.split(key, 6)
        s = 0.02
        return {'x': jax.random.normal(ks[0], (B, T, DIM), jnp.float32), 'wq': jax.random.normal(ks[1], (N_HEADS * HEAD_DIM, DIM), jnp.float32) * s, 'wk': jax.random.normal(ks[2], (N_KV_HEADS * HEAD_DIM, DIM), jnp.float32) * s, 'wv': jax.random.normal(ks[3], (N_KV_HEADS * HEAD_DIM, DIM), jnp.float32) * s, 'wo': jax.random.normal(ks[4], (DIM, N_HEADS * HEAD_DIM), jnp.float32) * s, 'q_norm_w': jnp.ones((N_HEADS * HEAD_DIM,), jnp.float32), 'k_norm_w': jnp.ones((N_KV_HEADS * HEAD_DIM,), jnp.float32)}
    _L0_attn_in = _L0_attn_setup()

    def _L0_ffn_setup():
        import jax, jax.numpy as jnp
        import numpy as np
        HIDDEN = 512
        INTER = 1408
        B, S = (2, 512)

        def _ternary(key, shape):
            return jax.random.randint(key, shape, -1, 2).astype(jnp.float32)
        key = jax.random.key(seed)
        ks = jax.random.split(key, 7)
        x = jax.random.normal(ks[0], (B, S, HIDDEN), dtype=jnp.float32)
        gate_w = _ternary(ks[1], (INTER, HIDDEN))
        up_w = _ternary(ks[2], (INTER, HIDDEN))
        down_w = _ternary(ks[3], (HIDDEN, INTER))
        gate_s = jax.random.uniform(ks[4], (INTER,), minval=0.01, maxval=0.1, dtype=jnp.float32)
        up_s = jax.random.uniform(ks[5], (INTER,), minval=0.01, maxval=0.1, dtype=jnp.float32)
        down_s = jax.random.uniform(ks[6], (HIDDEN,), minval=0.01, maxval=0.1, dtype=jnp.float32)
        return {'x': x, 'gate_w': gate_w, 'up_w': up_w, 'down_w': down_w, 'gate_s': gate_s, 'up_s': up_s, 'down_s': down_s}
    _L0_ffn_in = _L0_ffn_setup()
    _d = {'L0_attn_x': _L0_attn_in['x'], 'L0_attn_wq': _L0_attn_in['wq'], 'L0_attn_wk': _L0_attn_in['wk'], 'L0_attn_wv': _L0_attn_in['wv'], 'L0_attn_wo': _L0_attn_in['wo'], 'L0_attn_q_norm_w': _L0_attn_in['q_norm_w'], 'L0_attn_k_norm_w': _L0_attn_in['k_norm_w'], 'L0_ffn_gate_w': _L0_ffn_in['gate_w'], 'L0_ffn_up_w': _L0_ffn_in['up_w'], 'L0_ffn_down_w': _L0_ffn_in['down_w'], 'L0_ffn_gate_s': _L0_ffn_in['gate_s'], 'L0_ffn_up_s': _L0_ffn_in['up_s'], 'L0_ffn_down_s': _L0_ffn_in['down_s']}
    _x0 = _d['L0_attn_x']
    _d['L0_attn_x'] = jax.random.normal(jax.random.fold_in(jax.random.key(seed), 1), (4, 512, 512), dtype=_x0.dtype)
    del _x0
    return _d

def reference(L0_attn_x, L0_attn_wq, L0_attn_wk, L0_attn_wv, L0_attn_wo, L0_attn_q_norm_w, L0_attn_k_norm_w, L0_ffn_gate_w, L0_ffn_up_w, L0_ffn_down_w, L0_ffn_gate_s, L0_ffn_up_s, L0_ffn_down_s):

    def _L0_attn_ref(x, wq, wk, wv, wo, q_norm_w, k_norm_w):
        import jax, jax.numpy as jnp
        import numpy as np
        DIM = 512
        N_HEADS = 32
        N_KV_HEADS = 8
        HEAD_DIM = 64
        REPEATS = N_HEADS // N_KV_HEADS
        SLIDING_WINDOW = 256
        EPS = 1e-06
        B, T = (2, 512)

        def _alibi_slopes(n):
            r = 2.0 ** (-8.0 / n)
            return jnp.asarray([r ** i for i in range(n)], dtype=jnp.float32)

        def _rms_norm(x, w, eps):
            var = jnp.mean(x * x, axis=-1, keepdims=True)
            return x * jax.lax.rsqrt(var + eps) * w
        bsz, seqlen, _ = x.shape
        xq = _rms_norm(x @ wq.T, q_norm_w, EPS)
        xk = _rms_norm(x @ wk.T, k_norm_w, EPS)
        xv = x @ wv.T
        xq = xq.reshape(bsz, seqlen, N_HEADS, HEAD_DIM).transpose(0, 2, 1, 3)
        xk = xk.reshape(bsz, seqlen, N_KV_HEADS, HEAD_DIM).transpose(0, 2, 1, 3)
        xv = xv.reshape(bsz, seqlen, N_KV_HEADS, HEAD_DIM).transpose(0, 2, 1, 3)
        xk = jnp.repeat(xk, REPEATS, axis=1)
        xv = jnp.repeat(xv, REPEATS, axis=1)
        pos = jnp.arange(seqlen)
        dist = pos[None, :] - pos[:, None]
        slopes = _alibi_slopes(N_HEADS)
        alibi = slopes[:, None, None] * dist.astype(jnp.float32)
        allowed = (dist <= 0) & (dist >= -SLIDING_WINDOW)
        bias = jnp.where(allowed[None], alibi, -jnp.inf)
        scale = 1.0 / jnp.sqrt(jnp.asarray(HEAD_DIM, jnp.float32))
        scores = jnp.einsum('bhtd,bhsd->bhts', xq, xk) * scale + bias[None]
        attn = jax.nn.softmax(scores, axis=-1)
        out = jnp.einsum('bhts,bhsd->bhtd', attn, xv)
        out = out.transpose(0, 2, 1, 3).reshape(bsz, seqlen, N_HEADS * HEAD_DIM)
        return out @ wo.T

    def _L0_ffn_ref(x, gate_w, up_w, down_w, gate_s, up_s, down_s):
        import jax, jax.numpy as jnp
        import numpy as np
        HIDDEN = 512
        INTER = 1408
        B, S = (2, 512)

        def _ternary(key, shape):
            return jax.random.randint(key, shape, -1, 2).astype(jnp.float32)
        b, s, h = x.shape
        xf = x.reshape(b * s, h)
        g = jnp.einsum('th,ih->ti', xf, gate_w) * gate_s
        u = jnp.einsum('th,ih->ti', xf, up_w) * up_s
        hdn = jax.nn.silu(g) * u
        out = jnp.einsum('ti,hi->th', hdn, down_w) * down_s
        return out.reshape(b, s, -1)
    x = L0_attn_x
    x = x + _layernorm(_L0_attn_ref(_layernorm(x, axis=-1), L0_attn_wq, L0_attn_wk, L0_attn_wv, L0_attn_wo, L0_attn_q_norm_w, L0_attn_k_norm_w), axis=-1)
    x = x + _layernorm(_L0_ffn_ref(_layernorm(x, axis=-1), L0_ffn_gate_w, L0_ffn_up_w, L0_ffn_down_w, L0_ffn_gate_s, L0_ffn_up_s, L0_ffn_down_s), axis=-1)
    return x

_drawn_inputs = setup_inputs


def setup_inputs(seed=0):
    import zlib

    import numpy as np

    out = dict(_drawn_inputs(seed))
    spreads = {'L0_attn_q_norm_w': (1.0, 0.2), 'L0_attn_k_norm_w': (1.0, 0.2)}
    factors = {}
    for name, (base, spread) in spreads.items():
        noise = np.random.default_rng([zlib.crc32(name.encode()), seed]).standard_normal(out[name].shape)
        drawn = base * np.exp(spread * noise) if base else spread * noise
        out[name] = jnp.asarray(drawn.astype(out[name].dtype))
    for name, factor in factors.items():
        out[name] = (out[name] * factor).astype(out[name].dtype)
    return out
```

```python
from contextlib import ExitStack

import concourse.bass as bass
import numpy as np
from concourse import mybir

F32 = mybir.dt.float32
F32R = mybir.dt.float32r
F16 = mybir.dt.float16
ACT = mybir.ActivationFunctionType
ALU = mybir.AluOpType

P = 128
B, T, D = 4, 512, 512
H, G, HD = 32, 8, 64
REP = H // G
WINDOW = 256
INTER = 1408
KC = D // P
TT = T // P
QC, KVC = H * HD // P, G * HD // P
WQKV = (H + 2 * G) * HD
NB = WINDOW // P + 1
WIN = NB * P
IC = INTER // P
RMS_EPS, LN_EPS = 1e-6, 1e-5
BIG = 1e30
VSCALE = 1024.0
NGEMM = QC + KVC + TT
NSQ = QC + KVC - 2
WBLOCKS = WQKV // T
UNITS = 2 * TT * REP
LAG = TT + 1
STEP = 6
START = 2
RING = 4
PIECE = 3
DMA = 16
RATIO = 2.0 ** (-8.0 / H)
TINY = 1e-30
CONSTANTS = 6


def projection_schedule():
    k0, q = QC, iter(range(QC))
    order = [("gemm", n) for n in range(k0 + 2)] + [("root", 0)]
    for n, count in zip(range(k0 + 2, NGEMM), (3, 3, 3, 3, 2, 2)):
        order += [("norm", next(q)) for _ in range(count)] + [("gemm", n)]
        if n == k0 + KVC + 1:
            order.append(("root", 1))
    return order + [("norm", f) for f in range(QC, QC + KVC)]


def feed_forward_pieces():
    return [(kind, c, min(PIECE, IC - c)) for c in range(0, IC, PIECE) for kind in ("gate", "up", "down")]


SCHEDULE = projection_schedule()
PIECES = feed_forward_pieces()


def attention_loops(eng, attend):
    attend(0)
    with eng.Fori(1, LAG) as n:
        attend(n)
    attend(LAG, 0)
    with eng.Fori(1, TT) as i:
        attend(LAG + i, i)
    with eng.Fori(0, TT) as i:
        attend(LAG + TT + i, TT + i)
    with eng.Fori(0, TT - 1) as i:
        attend(LAG + 2 * TT + i, 2 * TT + i)


def at_least(eng, sem, value):
    if isinstance(value, int) and value <= 0:
        return
    eng.wait_ge(sem, value)


def part_products(a_hi, a_lo, b_hi, b_lo):
    return ((a_hi, b_hi), (a_lo, b_hi), (a_hi, b_lo))


def window(i):
    first = max(0, i - NB + 1)
    return first, i - first + 1, (first - i + NB - 1) * P


def qk_stores(b, f):
    per_q, per_k = 2 * DMA, 4 * DMA
    in_batch = per_q * (f // 2) if f < QC else per_q * (QC // 2) + per_k * ((f - QC) // 2)
    return (per_q * (QC // 2) + per_k * (KVC // 2)) * b + in_batch


def sandwich_layer(nc, x, wqT, wkT, wvT, woT, q_norm, k_norm, gateT, upT, downT, gate_s, up_s, down_s, out):
    x_t = x.rearrange("b (i p) d -> b p i d", p=P)
    out_t = out.rearrange("b (i p) d -> b p i d", p=P)
    x_flat = x.rearrange("b (i p) d -> (b i) p d", p=P)

    q_scr = nc.dram_tensor("q_scr", [B * H, HD, 2, T], F32, kind="Internal").ap()
    k_scr = nc.dram_tensor("k_scr", [B * G, HD, 2, 2, T], F32, kind="Internal").ap()
    v_scr = nc.dram_tensor("v_scr", [B * G, P, TT, 2 * HD], F16, kind="Internal").ap()
    o_scr = nc.dram_tensor("o_scr", [B * TT, TT, P, 2 * REP * HD], F32, kind="Internal").ap()
    vn_scr = nc.dram_tensor("vn_scr", [P, G * HD], F32, kind="Internal").ap()
    z_scr = nc.dram_tensor("z_scr", [B * TT, P, D], F32, kind="Internal").ap()

    with ExitStack() as ctx:
        def sb(scope, name, shape, dt=F32):
            return scope.enter_context(nc.sbuf_tensor(name, shape, dt))

        def sem(name):
            return ctx.enter_context(nc.semaphore(name))

        def sems(names):
            return [sem(name) for name in names.split()]

        bank = [ctx.enter_context(nc.psum_tensor(f"bank{i}", [P, 512], F32)) for i in range(8)]

        ident = sb(ctx, "ident", [P, P])
        ones = sb(ctx, "ones", [P, P])
        stats = sb(ctx, "stats", [P, TT, 6])
        moments = sb(ctx, "moments", [P, TT, 2])
        var_eps = sb(ctx, "var_eps", [P, TT])
        rstd = sb(ctx, "rstd", [P, TT])
        minus_half = sb(ctx, "minus_half", [P, TT])
        eps_rms = sb(ctx, "eps_rms", [P, 1])
        eps_tiny = sb(ctx, "eps_tiny", [P, 1])
        warm = sb(ctx, "warm", [P, 1])

        with ExitStack() as s1:
            w_hi = sb(s1, "w_hi", [P, KC, WQKV], F32R)
            w_lo = sb(s1, "w_lo", [P, KC, WQKV], F32R)
            w_stage = sb(s1, "w_stage", [P, 2, KC, T])
            xT_hi = sb(s1, "xT_hi", [P, KC, T], F32R)
            xT_lo = sb(s1, "xT_lo", [P, KC, T], F32R)
            x_in = sb(s1, "x_in", [P, TT, D])
            raw = sb(s1, "raw", [P, QC + KVC, T])
            square = sb(s1, "square", [P, 2, T])
            sum_sq = sb(s1, "sum_sq", [P, 2, T])
            inv_rms = sb(s1, "inv_rms", [P, 2, T])
            qk_hi = sb(s1, "qk_hi", [P, 2, T], F32R)
            qk_lo = sb(s1, "qk_lo", [P, 2, T], F32R)
            v_out = sb(s1, "v_out", [P, G, 2, HD], F16)
            qn_raw = sb(s1, "qn_raw", [P, QC])
            norm_w = sb(s1, "norm_w", [P, QC + KVC])

        with ExitStack() as s2:
            wo_hi = sb(s2, "wo_hi", [P, QC, D], F32R)
            wo_lo = sb(s2, "wo_lo", [P, QC, D], F32R)
            wo_stage = sb(s2, "wo_stage", [P, 2, D])
            q_st = sb(s2, "q_st", [P, 2, REP, T], F32R)
            k_st = sb(s2, "k_st", [P, 2, 2, T], F32R)
            v_st = sb(s2, "v_st", [P, 2, TT, 2 * HD], F16)
            dist = sb(s2, "dist", [P, WIN])
            slopes = sb(s2, "slopes", [P, H + 4 * REP])
            v_norm = sb(s2, "v_norm", [P, G + 2, HD])
            bias = sb(s2, "bias", [P, 2, REP, WIN])
            u_sb = sb(s2, "u_sb", [P, RING, WIN])
            low = sb(s2, "low", [P, RING])
            p_sb = sb(s2, "p_sb", [P, RING, WIN])
            pT_hi = sb(s2, "pT_hi", [P, RING, WIN], F16)
            pT_lo = sb(s2, "pT_lo", [P, RING, WIN], F16)
            p_sum = sb(s2, "p_sum", [P, TT, REP])
            inv_sum = sb(s2, "inv_sum", [P, 2, REP])
            o_low = sb(s2, "o_low", [P, REP, HD])
            o_raw = sb(s2, "o_raw", [P, 2, REP, HD])
            o_mid = sb(s2, "o_mid", [P, REP, HD])
            o_out = sb(s2, "o_out", [P, 2, REP, HD])
            o_in = sb(s2, "o_in", [P, TT, 2 * REP * HD])
            oT_hi = sb(s2, "oT_hi", [P, 2, 4, P], F32R)
            oT_lo = sb(s2, "oT_lo", [P, 2, 4, P], F32R)
            x_res = sb(s2, "x_res", [P, D])
            y_n = sb(s2, "y_n", [P, D])
            z_out = sb(s2, "z_out", [P, D])

        with ExitStack() as s4:
            gu_hi = sb(s4, "gu_hi", [P, KC, 2, INTER], F32R)
            gu_lo = sb(s4, "gu_lo", [P, KC, 2, INTER], F32R)
            dn_hi = sb(s4, "dn_hi", [P, IC, D], F32R)
            dn_lo = sb(s4, "dn_lo", [P, IC, D], F32R)
            f_stage = sb(s4, "f_stage", [P, 2, KC * PIECE * P])
            zT_hi = sb(s4, "zT_hi", [P, KC, T], F32R)
            zT_lo = sb(s4, "zT_lo", [P, KC, T], F32R)
            z_in = sb(s4, "z_in", [P, TT, D])
            silu = sb(s4, "silu", [P, T])
            hid = sb(s4, "hid", [P, T])
            h_hi = sb(s4, "h_hi", [P, 2, T], F32R)
            h_lo = sb(s4, "h_lo", [P, 2, T], F32R)
            y_s = sb(s4, "y_s", [P, TT, D])
            z_res = sb(s4, "z_res", [P, TT, D])
            gate_sc = sb(s4, "gate_sc", [P, IC])
            up_sc = sb(s4, "up_sc", [P, IC])
            down_sc = sb(s4, "down_sc", [P, D])

        const_ready, x_loaded, norm_loaded, norm_ready, vn_stored = sems(
            "const_ready x_loaded norm_loaded norm_ready vn_stored")
        w_loaded = sems("w_loaded0 w_loaded1")
        w_hi_ready, w_ready, v_squared, v_norm_psum, v_norm_ready, v_inv_ready, v_scaled = sems(
            "w_hi_ready w_ready v_squared v_norm_psum v_norm_ready v_inv_ready v_scaled")
        ln_stats, ln_moments, ln_var, ln_rstd, ln_done = sems("ln_stats ln_moments ln_var ln_rstd ln_done")
        xT_psum, xT_hi_ready, xT_ready, gemm_done = sems("xT_psum xT_hi_ready xT_ready gemm_done")
        raw_ready, sq_ready, acc_ready, ssq_psum, root_ready, inv_ready = sems(
            "raw_ready sq_ready acc_ready ssq_psum root_ready inv_ready")
        scaled, qk_hi_ready, qk_ready, v_hi_ready, v_ready, v_stored = sems(
            "scaled qk_hi_ready qk_ready v_hi_ready v_ready v_stored")
        qk_stored = sems("qk_stored0 qk_stored1")
        held = sem("held")
        heads_loaded, o_stored, wo_loaded = sems("heads_loaded0 heads_loaded1"), sems("o_stored0 o_stored1"), sems("wo_loaded0 wo_loaded1")
        dist_ready, bias_ready, vn_loaded = sems("dist_ready bias_ready vn_loaded")
        s_psum, u_ready, p_ready, pT_psum, pT_hi_ready, pT_ready, pv_done = sems(
            "s_psum u_ready p_ready pT_psum pT_hi_ready pT_ready pv_done")
        inv_sum_ready, o_low_ready, o_raw_ready, o_mid_ready, o_ready = sems(
            "inv_sum_ready o_low_ready o_raw_ready o_mid_ready o_ready")
        wo_hi_ready, wo_ready, tile_loaded, res1_loaded, oT_psum, oT_hi_ready, oT_ready, oT_used = sems(
            "wo_hi_ready wo_ready tile_loaded res1_loaded oT_psum oT_hi_ready oT_ready oT_used")
        y_stats, y_moments, y_var, y_rstd, y_normed, z_ready, z_stored = sems(
            "y_stats y_moments y_var y_rstd y_normed z_ready z_stored")
        f_loaded = sems("f_loaded0 f_loaded1")
        f_hi_ready, f_ready, scales_loaded, z_loaded, z_stats, z_moments, z_var, z_rstd, z_normed = sems(
            "f_hi_ready f_ready scales_loaded z_loaded z_stats z_moments z_var z_rstd z_normed")
        zT_psum, zT_hi_ready, zT_ready, gu_psum, silu_ready, hid_ready, h_hi_ready, h_ready = sems(
            "zT_psum zT_hi_ready zT_ready gu_psum silu_ready hid_ready h_hi_ready h_ready")
        down_done, ys_ready, f_stats, f_moments, f_var, f_rstd, f_normed, f_sum, res_loaded, out_stored = sems(
            "down_done ys_ready f_stats f_moments f_var f_rstd f_normed f_sum res_loaded out_stored")

        def piece(j):
            kind, at, size = PIECES[j]
            if kind == "down":
                src = f_stage[:, j % 2, 0:size * D].rearrange("p (c d) -> p c d", c=size)
                return src, dn_hi[:, at:at + size], dn_lo[:, at:at + size]
            src = f_stage[:, j % 2, 0:KC * P * size].rearrange("p (k n) -> p k n", k=KC)
            g = ("gate", "up").index(kind)
            return (src, *(w[:, :, g, P * at:P * (at + size)] for w in (gu_hi, gu_lo)))

        block = ctx.enter_context(nc.Block())

        def hold(eng):
            eng.sem_inc(held, 1)

        @block.sync
        def _(sp):
            w_src = [wqT[:, T * j:T * j + T] for j in range(H * HD // T)] + [wkT, wvT]

            def load_weights(j):
                at_least(sp, w_ready, j - 1)
                sp.dma_start(w_stage[:, j % 2], w_src[j].rearrange("(k p) n -> p k n", p=P)).then_inc(w_loaded[j % 2], DMA)

            sp.dma_start(x_in[:], x_t[0]).then_inc(x_loaded, DMA)
            load_weights(0)
            sp.dma_start(qn_raw[:], q_norm).then_inc(norm_loaded, DMA)
            sp.dma_start(norm_w[:, QC:], k_norm).then_inc(norm_loaded, DMA)
            for j in range(1, WBLOCKS):
                load_weights(j)

            def project(b, last=False):
                if not last:
                    sp.wait_ge(xT_psum, KC * b + KC)
                    sp.dma_start(x_in[:], x_t[bass.ds(b + 1, 1)].rearrange("a p i d -> p (a i) d")).then_inc(x_loaded, DMA)
                for kind, n in SCHEDULE:
                    if kind == "gemm" and n == QC and isinstance(b, int) and b == 0:
                        sp.wait_ge(v_norm_ready, 1)
                        sp.dma_start(vn_scr, raw[:, QC + KVC - 1]).then_inc(vn_stored, DMA)
                    if kind == "gemm" and n >= QC + KVC:
                        i = n - QC - KVC
                        sp.wait_ge(v_ready, TT * b + i + 1)
                        sp.dma_start(v_scr[bass.ds(b * G, G), :, i].rearrange("g p n -> p g n"),
                                     v_out[:].rearrange("p g t d -> p g (t d)")).then_inc(v_stored, DMA)
                    if kind == "norm":
                        sp.wait_ge(qk_ready, (QC + KVC) * b + n + 1)
                        for part, tile in enumerate((qk_hi, qk_lo)):
                            src = tile[:, n % 2].bitcast(F32)
                            if n < QC:
                                sp.dma_start(q_scr[bass.ds(b * H + 2 * n, 2), :, part].rearrange("h d n -> (h d) n"), src).then_inc(qk_stored[n % 2], DMA)
                            else:
                                for copy in range(2):
                                    sp.dma_start(k_scr[bass.ds(b * G + 2 * (n - QC), 2), :, copy, part].rearrange("h d n -> (h d) n"), src).then_inc(qk_stored[n % 2], DMA)

            project(0)
            with sp.Fori(1, B - 1) as b:
                project(b)
            project(B - 1, last=True)

            def stage1_stored(eng):
                for s in range(2):
                    eng.wait_ge(qk_stored[s], qk_stores(B, 0))
                eng.wait_ge(v_stored, DMA * B * TT)
                eng.wait_ge(vn_stored, DMA)

            stage1_stored(sp)

            def load_heads(n, s):
                at_least(sp, pv_done, UNITS * (n - 1) + UNITS // 2 * (s + 1))
                g = 2 * n + s
                sp.dma_start(k_st[:, s].bitcast(F32),
                             k_scr[bass.ds(g, 1)].rearrange("a d c t n -> (a d c) t n")).then_inc(heads_loaded[s], DMA)
                sp.dma_start(q_st[:, s].bitcast(F32),
                             q_scr[bass.ds(g * REP, REP)].rearrange("h d t n -> (d t) h n")).then_inc(heads_loaded[s], DMA)
                sp.dma_start(v_st[:, s],
                             v_scr[bass.ds(g, 1)].rearrange("a p i n -> (a p) i n")).then_inc(heads_loaded[s], DMA)

            def store_o(n, s, tiles):
                for i in tiles:
                    sp.wait_ge(o_ready, 2 * TT * n + TT * s + i + 1)
                    sp.dma_start(o_scr[bass.ds(n, 1), i, :, s * REP * HD:(s + 1) * REP * HD].rearrange("a p c -> (a p) c"),
                                 o_out[:, i % 2].rearrange("p r d -> p (r d)")).then_inc(o_stored[i % 2], DMA)

            def load_o(b, i):
                at_least(sp, oT_psum, 4 * (TT * b + i))
                sp.dma_start(o_in[:], o_scr[bass.ds(b * TT, TT), bass.ds(i, 1)].rearrange("g a p c -> p (g a) c")).then_inc(tile_loaded, DMA)

            def load_residual(t):
                at_least(sp, z_ready, t)
                sp.dma_start(x_res[:], x_flat[bass.ds(t, 1)].rearrange("a p d -> (a p) d")).then_inc(res1_loaded, DMA)

            def store_z(t):
                sp.wait_ge(z_ready, t + 1)
                sp.dma_start(z_scr[bass.ds(t, 1)].rearrange("a p d -> (a p) d"), z_out[:]).then_inc(z_stored, DMA)

            def attend(n, tile=None):
                load_heads(n, 0)
                if tile is not None:
                    for k in range(2):
                        sp.wait_ge(o_stored[k], DMA * (4 * (n - 1) + 2 - k))
                    hold(sp)
                    load_o(*tile)
                store_o(n - 1, 0, [TT - 1])
                store_o(n - 1, 1, range(TT - 1))
                load_heads(n, 1)
                store_o(n - 1, 1, [TT - 1])
                store_o(n, 0, [0])
                if tile is not None:
                    t = TT * tile[0] + tile[1]
                    if not isinstance(t, int):
                        store_z(t - 1)
                    load_residual(t)
                store_o(n, 0, range(1, TT - 1))

            load_heads(0, 0)
            load_heads(0, 1)
            sp.dma_start(v_norm[:, 0:G].rearrange("p g d -> p (g d)"), vn_scr).then_inc(vn_loaded, DMA)
            sp.dma_start(v_norm[:, G:G + 2].rearrange("p g d -> p (g d)"), vn_scr[:, 0:2 * HD]).then_inc(vn_loaded, DMA)
            for i in range(TT):
                for c in range(QC // TT * i, QC // TT * (i + 1)):
                    at_least(sp, wo_ready, c - 1)
                    sp.dma_start(wo_stage[:, c % 2], woT[P * c:P * c + P, :]).then_inc(wo_loaded[c % 2], DMA)
                if i < TT - 1:
                    store_o(0, 0, [i])
            with sp.Fori(1, LAG) as n:
                attend(n)
            attend(LAG, (0, 0))
            with sp.Fori(1, TT) as i:
                attend(LAG + i, (0, i))
            with sp.Fori(0, TT) as i:
                attend(LAG + TT + i, (1, i))
            with sp.Fori(0, TT - 1) as i:
                attend(LAG + 2 * TT + i, (2, i))
            store_o(B * TT - 1, 0, [TT - 1])
            store_o(B * TT - 1, 1, range(TT))
            for k in range(2):
                sp.wait_ge(o_stored[k], DMA * 4 * B * TT)
            load_o(B - 2, TT - 1)
            with sp.Fori(0, TT) as i:
                store_z(TT * (B - 1) + i - 2)
                load_residual(TT * (B - 1) + i - 1)
                load_o(B - 1, i)
            store_z(B * TT - 2)
            load_residual(B * TT - 1)
            store_z(B * TT - 1)
            sp.wait_ge(z_stored, DMA * B * TT)

            def load_z(tile, m, done):
                sp.dma_start(tile[:], z_scr[bass.ds(TT * m, TT)].rearrange("i p d -> p i d")).then_inc(done, DMA)

            load_z(z_in, 0, z_loaded)
            sp.dma_start(gate_sc[:], gate_s).then_inc(scales_loaded, DMA)
            sp.dma_start(up_sc[:], up_s).then_inc(scales_loaded, DMA)
            sp.dma_start(down_sc[:], down_s.partition_broadcast(P)).then_inc(scales_loaded, DMA)
            for j, (kind, at, size) in enumerate(PIECES):
                at_least(sp, f_ready, j - 1)
                if kind == "down":
                    src = downT[P * at:P * (at + size), :].rearrange("(c p) d -> p c d", p=P)
                    dst = f_stage[:, j % 2, 0:size * D].rearrange("p (c d) -> p c d", c=size)
                else:
                    src = (gateT if kind == "gate" else upT)[:, P * at:P * (at + size)].rearrange("(k p) n -> p k n", p=P)
                    dst = f_stage[:, j % 2, 0:KC * P * size].rearrange("p (k n) -> p k n", k=KC)
                sp.dma_start(dst, src).then_inc(f_loaded[j % 2], DMA)

            def feed_forward(m, last=False):
                if not last:
                    sp.wait_ge(zT_psum, KC * m + KC)
                    load_z(z_in, m + 1, z_loaded)
                at_least(sp, f_sum, TT * m)
                load_z(z_res, m, res_loaded)
                sp.wait_ge(f_sum, TT * m + TT)
                sp.dma_start(out_t[bass.ds(m, 1)].rearrange("a p i d -> p (a i) d"), y_s[:]).then_inc(out_stored, DMA)

            feed_forward(0)
            with sp.Fori(1, B - 1) as m:
                feed_forward(m)
            feed_forward(B - 1, last=True)
            sp.wait_ge(out_stored, DMA * B)

        @block.gpsimd
        def _(pool):
            nc.gpsimd.memset(ident[:], 0.0).then_inc(const_ready, 1)
            nc.gpsimd.memset(ones[:], 1.0).then_inc(const_ready, 1)
            nc.gpsimd.memset(minus_half[:], -0.5).then_inc(const_ready, 1)
            nc.gpsimd.memset(eps_rms[:], RMS_EPS).then_inc(const_ready, 1)
            nc.gpsimd.memset(eps_tiny[:], TINY).then_inc(const_ready, 1)
            pool.wait_ge(const_ready, 5)
            nc.gpsimd.affine_select(out=ident[:], in_=ident[:], compare_op=ALU.not_equal, fill=1.0, base=0,
                                    pattern=[[-1, P]], channel_multiplier=1).then_inc(const_ready, 1)

            def inverse_root(count, var_ready, value, done):
                pool.wait_ge(var_ready, value)
                nc.gpsimd.tensor_tensor(out=rstd[:, 0:count], in0=var_eps[:, 0:count], in1=minus_half[:, 0:count],
                                        op=ALU.pow).then_inc(done, 1)

            with pool.Fori(0, B) as b:
                inverse_root(TT, ln_var, b + 1, ln_rstd)

            for s in range(2):
                pool.wait_ge(qk_stored[s], qk_stores(B, 0))
            pool.wait_ge(v_stored, DMA * B * TT)
            nc.gpsimd.iota(dist[:], pattern=[[-1, WIN]], base=WINDOW, channel_multiplier=1,
                           allow_small_or_imprecise_dtypes=True).then_inc(dist_ready, 1)
            for h in range(H + 4 * REP):
                nc.gpsimd.memset(slopes[:, h:h + 1], float(np.float32(RATIO ** (h % H)))).then_inc(dist_ready, 1)
            pool.wait_ge(dist_ready, 1 + H + 4 * REP)
            nc.gpsimd.affine_select(out=dist[:], in_=dist[:], compare_op=ALU.is_ge, fill=BIG, base=WINDOW,
                                    pattern=[[-1, WIN]], channel_multiplier=1).then_inc(dist_ready, 1)
            pool.wait_ge(dist_ready, 2 + H + 4 * REP)
            nc.gpsimd.affine_select(out=dist[:], in_=dist[:], compare_op=ALU.is_ge, fill=BIG, base=0,
                                    pattern=[[1, WIN]], channel_multiplier=-1).then_inc(dist_ready, 1)
            pool.wait_ge(dist_ready, 3 + H + 4 * REP)

            def make_bias(n, q, s):
                at_least(pool, u_ready, UNITS * (n - 1) + UNITS // 2 * (s + 1))
                hold(pool)
                nc.gpsimd.tensor_tensor(out=bias[:, s], in0=dist[:].unsqueeze(1).broadcast_to([P, REP, WIN]),
                                        in1=slopes[:, bass.ds(2 * REP * q + REP * s, REP)].unsqueeze(2).broadcast_to([P, REP, WIN]),
                                        op=ALU.mult).then_inc(bias_ready, 1)

            def finish_o(n, q, s, i):
                a = 2 * TT * n + TT * s + i
                pool.wait_ge(inv_sum_ready, a + 1)
                pool.wait_ge(o_raw_ready, a + 1)
                at_least(pool, o_ready, a)
                nc.gpsimd.tensor_tensor(out=o_mid[:], in0=o_raw[:, i % 2],
                                        in1=inv_sum[:, i % 2].unsqueeze(2).broadcast_to([P, REP, HD]),
                                        op=ALU.mult).then_inc(o_mid_ready, 1)
                pool.wait_ge(o_mid_ready, a + 1)
                at_least(pool, o_stored[i % 2], DMA * (TT * n + TT // 2 * s + i // 2))
                hold(pool)
                nc.gpsimd.tensor_tensor(out=o_out[:, i % 2], in0=o_mid[:],
                                        in1=v_norm[:, bass.ds(2 * q + s, 1)].broadcast_to([P, REP, HD]),
                                        op=ALU.mult).then_inc(o_ready, 1)

            def split_wo(c):
                pool.wait_ge(wo_loaded[c % 2], DMA * (c // 2 + 1))
                nc.gpsimd.tensor_copy(wo_hi[:, c], wo_stage[:, c % 2]).then_inc(wo_hi_ready, 1)
                pool.wait_ge(wo_hi_ready, c + 1)
                nc.gpsimd.tensor_tensor(out=wo_lo[:, c], in0=wo_stage[:, c % 2], in1=wo_hi[:, c].bitcast(F32),
                                        op=ALU.subtract).then_inc(wo_ready, 1)

            def add_residual(t):
                pool.wait_ge(y_normed, t + 1)
                pool.wait_ge(res1_loaded, DMA * (t + 1))
                at_least(pool, z_stored, DMA * t)
                nc.gpsimd.tensor_tensor(out=z_out[:], in0=y_n[:], in1=x_res[:], op=ALU.add).then_inc(z_ready, 1)

            def attend(n, q, tile=None):
                for i in range(TT // 2, TT):
                    finish_o(n - 1, q - 1, 1, i)
                make_bias(n, q, 1)
                for i in range(TT):
                    finish_o(n, q, 0, i)
                    if i == 0 and tile is not None and not (isinstance(tile, int) and tile == 0):
                        add_residual(tile - 1)
                make_bias(n + 1, q + 1, 0)
                for i in range(TT // 2):
                    finish_o(n, q, 1, i)
                if tile is not None:
                    inverse_root(1, y_var, tile + 1, y_rstd)

            make_bias(0, 0, 0)
            make_bias(0, 0, 1)
            pool.wait_ge(vn_loaded, 2 * DMA)
            for i in range(TT):
                for c in range(QC // TT * i, QC // TT * (i + 1)):
                    split_wo(c)
                finish_o(0, 0, 0, i)
            make_bias(1, 1, 0)
            for i in range(TT // 2):
                finish_o(0, 0, 1, i)
            with pool.Fori(1, LAG) as n:
                attend(n, n)
            attend(LAG, 1, 0)
            with pool.Fori(1, TT) as i:
                attend(LAG + i, i + 1, i)
            with pool.Fori(0, TT) as i:
                attend(LAG + TT + i, i + 1, TT + i)
            with pool.Fori(0, TT - 1) as i:
                attend(LAG + 2 * TT + i, i + 1, 2 * TT + i)
            for i in range(TT // 2, TT):
                finish_o(B * TT - 1, TT - 1, 1, i)
            add_residual(B * TT - LAG - 1)
            with pool.Fori(B * TT - LAG, B * TT) as t:
                inverse_root(1, y_var, t + 1, y_rstd)
                add_residual(t)

            inverse_root(TT, z_var, 1, z_rstd)

            def feed_forward(m, last=False):
                if not last:
                    inverse_root(TT, z_var, m + 2, z_rstd)
                inverse_root(TT, f_var, m + 1, f_rstd)
                pool.wait_ge(res_loaded, DMA * (m + 1))
                for i in range(TT):
                    pool.wait_ge(f_normed, TT * m + i + 1)
                    nc.gpsimd.tensor_tensor(out=y_s[:, i], in0=y_s[:, i], in1=z_res[:, i], op=ALU.add).then_inc(f_sum, 1)

            with pool.Fori(0, B - 1) as m:
                feed_forward(m)
            feed_forward(B - 1, last=True)

        @block.scalar
        def _(act):
            act.wait_ge(const_ready, CONSTANTS)
            nc.scalar.activation(warm[:], ones[:, 0:1], ACT.Sqrt)

            def round_xT(b):
                for kc in range(KC):
                    act.wait_ge(xT_psum, KC * b + kc + 1)
                    nc.scalar.activation(xT_hi[:, kc], bank[4 + kc % 2][:], ACT.Copy).then_inc(xT_hi_ready, 1)

            def norm_of_v():
                act.wait_ge(w_loaded[1], DMA * WBLOCKS // 2)
                for kc in range(KC):
                    nc.scalar.activation(raw[:, QC + kc], w_stage[:, 1, kc], ACT.Square).then_inc(v_squared, 1)
                act.wait_ge(v_norm_psum, 1)
                nc.scalar.activation(raw[:, QC + KVC - 1], bank[7][:], ACT.Sqrt, scale=VSCALE ** -2,
                                     bias=eps_tiny[:]).then_inc(v_norm_ready, 1)

            def project(b, last=False):
                first = isinstance(b, int) and b == 0
                for kind, n in SCHEDULE:
                    if kind == "norm":
                        act.wait_ge(scaled, (QC + KVC) * b + n + 1)
                        at_least(act, qk_stored[n % 2], qk_stores(b, n))
                        nc.scalar.activation(qk_hi[:, n % 2], raw[:, n], ACT.Copy).then_inc(qk_hi_ready, 1)
                    elif kind == "root":
                        act.wait_ge(ssq_psum, 2 * b + n + 1)
                        if first and n == 1:
                            act.wait_ge(v_scaled, 1)
                        nc.scalar.activation(inv_rms[:, n], bank[6 + n][:], ACT.Sqrt, scale=1.0 / (D if n else H * HD),
                                             bias=eps_rms[:]).then_inc(root_ready, 1)
                    elif kind == "gemm" and n < QC + KVC:
                        if first and n == QC:
                            norm_of_v()
                        if first and n == QC + KVC - 1:
                            act.wait_ge(vn_stored, DMA)
                            act.wait_ge(v_inv_ready, 1)
                        act.wait_ge(gemm_done, NGEMM * b + n + 1)
                        at_least(act, qk_ready, (QC + KVC) * (b - 1) + n + 1)
                        nc.scalar.activation(raw[:, n], bank[n % 4][:], ACT.Copy).then_inc(raw_ready, 1)
                        if n in (0, QC):
                            at_least(act, ssq_psum, 2 * (b - 1) + n // QC + 1)
                            dst = sum_sq[:, n // QC]
                        else:
                            m = n - 1 - n // QC
                            at_least(act, acc_ready, NSQ * b + m - 1)
                            dst = square[:, m % 2]
                        nc.scalar.activation(dst, bank[n % 4][:], ACT.Square).then_inc(sq_ready, 1)
                    elif kind == "gemm":
                        i = n - QC - KVC
                        act.wait_ge(gemm_done, NGEMM * b + n + 1)
                        at_least(act, v_stored, DMA * (TT * b + i))
                        nc.scalar.activation(v_out[:, :, 0], bank[n % 4][:].rearrange("p (g d) -> p g d", g=G),
                                             ACT.Copy).then_inc(v_hi_ready, 1)
                if not last:
                    round_xT(b + 1)

            round_xT(0)
            project(0)
            with act.Fori(1, B - 1) as b:
                project(b)
            project(B - 1, last=True)

            nc.scalar.activation(warm[:], ones[:, 0:1], ACT.Exp)

            def exps(n, u):
                A, i, r = UNITS * n + u, u // REP % TT, u % REP
                a, w = 2 * TT * n + u // REP, P * window(i)[1]
                act.wait_ge(u_ready, A + 1)
                at_least(act, pT_psum, A - RING + 1)
                if r == 0:
                    at_least(act, inv_sum_ready, a - TT + 1)
                nc.scalar.activation(p_sb[:, u % RING, 0:w], u_sb[:, u % RING, 0:w], ACT.Exp, scale=-1.0,
                                     bias=low[:, u % RING:u % RING + 1],
                                     accum_out=p_sum[:, i, r:r + 1]).then_inc(p_ready, 1)

            def round_pT(n, u):
                A, w = UNITS * n + u, P * window(u // REP % TT)[1]
                act.wait_ge(pT_psum, A + 1)
                at_least(act, pv_done, A - RING + 1)
                nc.scalar.activation(pT_hi[:, u % RING, 0:w], bank[2 + u % 2][:, 0:w], ACT.Copy).then_inc(pT_hi_ready, 1)

            def copy_low(n, u):
                act.wait_ge(pv_done, UNITS * n + u + 1)
                at_least(act, o_raw_ready, 2 * TT * n + u // REP)
                nc.scalar.activation(o_low[:], bank[4 + u // REP % 2][:].rearrange("p (r t d) -> p r t d", r=REP, t=2)[:, :, 1],
                                     ACT.Copy).then_inc(o_low_ready, 1)

            def round_oT(t, m):
                act.wait_ge(oT_psum, 4 * t + m + 1)
                at_least(act, oT_used, 4 * t + m - 1)
                nc.scalar.activation(oT_hi[:, m % 2].rearrange("p c n -> p (c n)"), bank[6][:], ACT.Copy).then_inc(oT_hi_ready, 1)

            def attend(n, tile=None):
                for u in range(UNITS):
                    for lag, work in ((2, round_pT), (0, exps), (5, copy_low)):
                        nn, uu = (n, u - lag) if u >= lag else (n - 1, UNITS + u - lag)
                        if not (isinstance(nn, int) and nn < 0) and (work is not copy_low or uu % REP == REP - 1):
                            work(nn, uu)
                    m, at = divmod(u - START - 1, STEP)
                    if tile is not None and m in range(4) and at == 0:
                        round_oT(tile, m)

            attention_loops(act, attend)
            round_pT(B * TT - 1, UNITS - 2)
            copy_low(B * TT - 1, UNITS - 1 - REP)
            round_pT(B * TT - 1, UNITS - 1)
            copy_low(B * TT - 1, UNITS - 1)

            with act.Fori(B * TT - LAG, B * TT) as t:
                for m in range(4):
                    round_oT(t, m)

            nc.scalar.activation(warm[:], ones[:, 0:1], ACT.Silu)

            def round_zT(m):
                for kc in range(KC):
                    act.wait_ge(zT_psum, KC * m + kc + 1)
                    nc.scalar.activation(zT_hi[:, kc], bank[kc][:], ACT.Copy).then_inc(zT_hi_ready, 1)

            def feed_forward(m, last=False):
                for c in range(IC):
                    C = IC * m + c
                    if isinstance(m, int) and m == 0 and c % PIECE == 0:
                        for j in range(c, c + 3):
                            kind, at, size = PIECES[j]
                            act.wait_ge(f_loaded[j % 2], DMA * (j // 2 + 1))
                            src, hi, _ = piece(j)
                            nc.scalar.activation(hi, src, ACT.Copy).then_inc(f_hi_ready, 1)
                    if isinstance(m, int) and m == 0 and c == 0:
                        act.wait_ge(scales_loaded, 3 * DMA)
                    act.wait_ge(gu_psum, 2 * C + 1)
                    at_least(act, hid_ready, C)
                    nc.scalar.activation(silu[:], bank[2 * (c % 2)][:], ACT.Silu, scale=gate_sc[:, c:c + 1]).then_inc(silu_ready, 1)
                    act.wait_ge(hid_ready, C + 1)
                    at_least(act, down_done, C - 1 + (c == 0))
                    nc.scalar.activation(h_hi[:, c % 2], hid[:], ACT.Copy).then_inc(h_hi_ready, 1)
                if not last:
                    round_zT(m + 1)

            round_zT(0)
            feed_forward(0)
            with act.Fori(1, B - 1) as m:
                feed_forward(m)
            feed_forward(B - 1, last=True)

        @block.vector
        def _(dve):
            def layer_stats(k, loaded, value, tiles, stats_ready, moments_ready, var_ready):
                count = len(tiles)
                dve.wait_ge(loaded, value)
                for i, tile in enumerate(tiles):
                    nc.vector.bn_stats(stats[:, i], tile).then_inc(stats_ready, 1)
                for i in range(count):
                    dve.wait_ge(stats_ready, count * k + i + 1)
                    hold(dve)
                    nc.vector.bn_aggr(moments[:, i], stats[:, i]).then_inc(moments_ready, 1)
                dve.wait_ge(moments_ready, count * k + count)
                nc.vector.tensor_scalar_add(var_eps[:, 0:count], moments[:, 0:count, 1], LN_EPS).then_inc(var_ready, 1)

            def layer_norm(k, dst, src, i, rstd_ready, normed):
                dve.wait_ge(rstd_ready, k + 1)
                nc.vector.tensor_scalar(dst, src, moments[:, i, 0:1], rstd[:, i:i + 1], ALU.subtract, ALU.mult).then_inc(normed, 1)

            def stats_x(b):
                layer_stats(b, x_loaded, DMA * (b + 1), [x_in[:, i] for i in range(TT)], ln_stats, ln_moments, ln_var)

            def norm_x(b):
                for i in range(TT):
                    layer_norm(b, x_in[:, i], x_in[:, i], i, ln_rstd, ln_done)

            def split_xT(b):
                for kc in range(KC):
                    dve.wait_ge(xT_hi_ready, KC * b + kc + 1)
                    nc.vector.tensor_tensor(xT_lo[:, kc], bank[4 + kc % 2][:], xT_hi[:, kc].bitcast(F32), ALU.subtract).then_inc(xT_ready, 1)

            def split_weights(j):
                hi, lo = (w[:, :, T * j:T * j + T] for w in (w_hi, w_lo))
                dve.wait_ge(w_loaded[j % 2], DMA * (j // 2 + 1))
                if j == WBLOCKS - 1:
                    dve.wait_ge(v_norm_ready, 1)
                    nc.vector.reciprocal(inv_rms[:, 1], raw[:, QC + KVC - 1]).then_inc(v_inv_ready, 1)
                    dve.wait_ge(v_inv_ready, 1)
                    nc.vector.tensor_tensor(w_stage[:, 1], w_stage[:, 1], inv_rms[:, 1:2].broadcast_to([P, KC, T]), ALU.mult).then_inc(v_scaled, 1)
                    dve.wait_ge(v_scaled, 1)
                nc.vector.tensor_copy(hi, w_stage[:, j % 2]).then_inc(w_hi_ready, 1)
                dve.wait_ge(w_hi_ready, j + 1)
                nc.vector.tensor_tensor(lo, w_stage[:, j % 2], hi.bitcast(F32), ALU.subtract).then_inc(w_ready, 1)

            def split_raw(b, f):
                dve.wait_ge(qk_hi_ready, (QC + KVC) * b + f + 1)
                nc.vector.tensor_tensor(qk_lo[:, f % 2], raw[:, f], qk_hi[:, f % 2].bitcast(F32), ALU.subtract).then_inc(qk_ready, 1)

            def project(b, last=False):
                first = isinstance(b, int) and b == 0
                for kind, n in SCHEDULE:
                    if kind == "norm":
                        dve.wait_ge(inv_ready, 2 * b + n // QC + 1)
                        nc.vector.scalar_tensor_tensor(raw[:, n], raw[:, n], norm_w[:, n:n + 1], inv_rms[:, n // QC],
                                                       ALU.mult, ALU.mult).then_inc(scaled, 1)
                        if n not in (0, QC):
                            split_raw(b, n - 1)
                        if n in (QC - 1, QC + KVC - 1):
                            split_raw(b, n)
                    elif kind == "root":
                        dve.wait_ge(root_ready, 2 * b + n + 1)
                        nc.vector.reciprocal(inv_rms[:, n], inv_rms[:, n]).then_inc(inv_ready, 1)
                    elif n < QC + KVC:
                        if first and n % 4 == 0:
                            split_weights(n // 4)
                        if first and n == QC + 2:
                            split_weights(WBLOCKS - 1)
                        if not last and n == QC:
                            stats_x(b + 1)
                        if n not in (0, QC):
                            m = n - 1 - n // QC
                            dve.wait_ge(sq_ready, (QC + KVC) * b + n + 1)
                            at_least(dve, acc_ready, NSQ * b + m)
                            nc.vector.tensor_tensor(sum_sq[:, n // QC], sum_sq[:, n // QC], square[:, m % 2], ALU.add).then_inc(acc_ready, 1)
                        if not last and n == QC + KVC - 1:
                            norm_x(b + 1)
                    else:
                        dve.wait_ge(v_hi_ready, TT * b + n - QC - KVC + 1)
                        nc.vector.tensor_tensor(v_out[:, :, 1], bank[n % 4][:].rearrange("p (g d) -> p g d", g=G), v_out[:, :, 0],
                                                ALU.subtract).then_inc(v_ready, 1)
                if not last:
                    split_xT(b + 1)

            stats_x(0)
            norm_x(0)
            dve.wait_ge(norm_loaded, 2 * DMA)
            nc.vector.tensor_scalar_mul(norm_w[:, 0:QC], qn_raw[:], -HD ** -0.5).then_inc(norm_ready, 1)
            split_xT(0)
            dve.wait_ge(norm_ready, 1)
            project(0)
            with dve.Fori(1, B - 1) as b:
                project(b)
            project(B - 1, last=True)

            def add_bias(n, u):
                A, i = UNITS * n + u, u // REP % TT
                _, tiles, at = window(i)
                w = P * tiles
                if u % (UNITS // 2) == 0:
                    dve.wait_ge(bias_ready, 2 * n + 2 * u // UNITS + 1)
                dve.wait_ge(s_psum, A + 1)
                at_least(dve, p_ready, A - RING + 1)
                hold(dve)
                nc.vector.tensor_tensor_reduce(out=u_sb[:, u % RING, 0:w], in0=bank[u % 2][:, 0:w],
                                               in1=bias[:, 2 * u // UNITS, u % REP, at:at + w], scale=1.0, scalar=BIG,
                                               op0=ALU.add, op1=ALU.min, accum_out=low[:, u % RING:u % RING + 1]).then_inc(u_ready, 1)

            def split_pT(n, u):
                w = P * window(u // REP % TT)[1]
                dve.wait_ge(pT_hi_ready, UNITS * n + u + 1)
                nc.vector.tensor_tensor(pT_lo[:, u % RING, 0:w], bank[2 + u % 2][:, 0:w], pT_hi[:, u % RING, 0:w],
                                        ALU.subtract).then_inc(pT_ready, 1)

            def invert_sums(n, u):
                a = 2 * TT * n + u // REP
                dve.wait_ge(p_ready, UNITS * n + u + 1)
                at_least(dve, o_mid_ready, a - 1)
                nc.vector.reciprocal(inv_sum[:, u // REP % 2], p_sum[:, u // REP % TT]).then_inc(inv_sum_ready, 1)

            def add_low(n, u):
                a = 2 * TT * n + u // REP
                dve.wait_ge(o_low_ready, a + 1)
                at_least(dve, o_mid_ready, a - 1)
                nc.vector.tensor_tensor(o_raw[:, u // REP % 2],
                                        bank[4 + u // REP % 2][:].rearrange("p (r t d) -> p r t d", r=REP, t=2)[:, :, 0],
                                        o_low[:], ALU.add).then_inc(o_raw_ready, 1)

            def split_oT(t, m):
                dve.wait_ge(oT_hi_ready, 4 * t + m + 1)
                nc.vector.tensor_tensor(oT_lo[:, m % 2].rearrange("p c n -> p (c n)"), bank[6][:],
                                        oT_hi[:, m % 2].rearrange("p c n -> p (c n)").bitcast(F32), ALU.subtract).then_inc(oT_ready, 1)

            def stats_y(t, acc):
                layer_stats(t, oT_used, 4 * t + 4, [acc[:]], y_stats, y_moments, y_var)

            def norm_y(t, acc):
                at_least(dve, z_ready, t)
                layer_norm(t, y_n[:], acc[:], 0, y_rstd, y_normed)

            def attend(n, tile=None):
                for u in range(UNITS):
                    add_bias(n, u)
                    for lag, work in ((2, split_pT), (1, invert_sums), (6, add_low)):
                        nn, uu = (n, u - lag) if u >= lag else (n - 1, UNITS + u - lag)
                        if not (isinstance(nn, int) and nn < 0) and (work is split_pT or uu % REP == REP - 1):
                            work(nn, uu)
                    m, at = divmod(u - START - 2, STEP)
                    if tile is not None and m in range(4) and at == 0:
                        split_oT(tile, m)
                    if u == START and tile is not None and not (isinstance(tile, int) and tile == 0):
                        norm_y(tile - 1, bank[7])
                if tile is not None:
                    stats_y(tile, bank[7])

            attention_loops(dve, attend)
            invert_sums(B * TT - 1, UNITS - 1)
            split_pT(B * TT - 1, UNITS - 2)
            add_low(B * TT - 1, UNITS - 1 - REP)
            split_pT(B * TT - 1, UNITS - 1)
            add_low(B * TT - 1, UNITS - 1)

            def finish_tile(t, acc, acc_before):
                for m in range(4):
                    split_oT(t, m)
                    if m == 0:
                        norm_y(t - 1, acc_before)
                stats_y(t, acc)

            finish_tile(B * TT - LAG, bank[5], bank[7])
            with dve.Fori(0, TT // 2) as i:
                finish_tile(B * TT - TT + 2 * i, bank[7], bank[5])
                finish_tile(B * TT - TT + 1 + 2 * i, bank[5], bank[7])
            norm_y(B * TT - 1, bank[5])

            def stats_z(m):
                layer_stats(m, z_loaded, DMA * (m + 1), [z_in[:, i] for i in range(TT)], z_stats, z_moments, z_var)

            def norm_z(m):
                for i in range(TT):
                    layer_norm(m, z_in[:, i], z_in[:, i], i, z_rstd, z_normed)

            def split_zT(m):
                for kc in range(KC):
                    dve.wait_ge(zT_hi_ready, KC * m + kc + 1)
                    nc.vector.tensor_tensor(zT_lo[:, kc], bank[kc][:], zT_hi[:, kc].bitcast(F32), ALU.subtract).then_inc(zT_ready, 1)

            def feed_forward(m, last=False):
                first = isinstance(m, int) and m == 0
                for c in range(IC):
                    C = IC * m + c
                    if first and c % PIECE == 0:
                        for j in range(c, c + 3):
                            src, hi, lo = piece(j)
                            dve.wait_ge(f_hi_ready, j + 1)
                            nc.vector.tensor_tensor(lo, src, hi.bitcast(F32), ALU.subtract).then_inc(f_ready, 1)
                    if not last and c == IC - 2:
                        stats_z(m + 1)
                    if not last and c == IC - 1:
                        norm_z(m + 1)
                    dve.wait_ge(gu_psum, 2 * C + 2)
                    dve.wait_ge(silu_ready, C + 1)
                    at_least(dve, h_ready, C)
                    nc.vector.scalar_tensor_tensor(hid[:], bank[2 * (c % 2) + 1][:], up_sc[:, c:c + 1], silu[:],
                                                   ALU.mult, ALU.mult).then_inc(hid_ready, 1)
                    dve.wait_ge(h_hi_ready, C + 1)
                    nc.vector.tensor_tensor(h_lo[:, c % 2], hid[:], h_hi[:, c % 2].bitcast(F32), ALU.subtract).then_inc(h_ready, 1)
                if not last:
                    split_zT(m + 1)
                dve.wait_ge(down_done, IC * (m + 1))
                at_least(dve, out_stored, DMA * m)
                for i in range(TT):
                    nc.vector.tensor_tensor(y_s[:, i], bank[4 + i][:], down_sc[:], ALU.mult).then_inc(ys_ready, 1)
                layer_stats(m, ys_ready, TT * (m + 1), [y_s[:, i] for i in range(TT)], f_stats, f_moments, f_var)
                for i in range(TT):
                    layer_norm(m, y_s[:, i], y_s[:, i], i, f_rstd, f_normed)

            stats_z(0)
            norm_z(0)
            split_zT(0)
            dve.wait_ge(scales_loaded, 3 * DMA)
            feed_forward(0)
            with dve.Fori(1, B - 1) as m:
                feed_forward(m)
            feed_forward(B - 1, last=True)

        @block.tensor
        def _(pe):
            pe.wait_ge(const_ready, CONSTANTS)

            def transpose_x(b):
                for kc in range(KC):
                    pe.wait_ge(ln_done, TT * b + TT)
                    at_least(pe, xT_ready, KC * b + kc - 1)
                    for i in range(TT):
                        last = nc.tensor.transpose(bank[4 + kc % 2][:, P * i:P * i + P], x_in[:, i, P * kc:P * kc + P], ident[:])
                    last.then_inc(xT_psum, 1)

            def sum_squares(b, n):
                pe.wait_ge(acc_ready, NSQ * b + (NSQ if n else QC - 1))
                pe.wait_ge(sq_ready, (QC + KVC) * b + (QC + KVC if n else QC))
                at_least(pe, root_ready, 2 * (b - 1) + n + 1)
                if n and isinstance(b, int) and b == 0:
                    pe.wait_ge(v_norm_ready, 1)
                nc.tensor.matmul(bank[6 + n][:], ones[:], sum_sq[:, n], start=True, stop=True).then_inc(ssq_psum, 1)

            def project(b, last=False):
                first = isinstance(b, int) and b == 0
                for n in range(NGEMM):
                    if first and n == QC:
                        for kc in range(KC):
                            pe.wait_ge(v_squared, kc + 1)
                            mm = nc.tensor.matmul(bank[7][:], ones[:], raw[:, QC + kc], start=(kc == 0), stop=(kc == KC - 1))
                        mm.then_inc(v_norm_psum, 1)
                    if first and n % 4 == 0:
                        pe.wait_ge(w_ready, n // 4 + 1)
                    if n < 4:
                        at_least(pe, v_ready, TT * (b - 1) + n + 1)
                    else:
                        pe.wait_ge(sq_ready, (QC + KVC) * b + n - 4 + 1)
                    for kc in range(KC):
                        if n == 0:
                            pe.wait_ge(xT_ready, KC * b + kc + 1)
                        if n < QC + KVC:
                            cols = slice(P * n, P * n + P)
                            parts = part_products(w_hi[:, kc, cols], w_lo[:, kc, cols], xT_hi[:, kc], xT_lo[:, kc])
                        else:
                            i = n - QC - KVC
                            tokens, cols = slice(P * i, P * i + P), slice(WQKV - G * HD, WQKV)
                            parts = part_products(xT_hi[:, kc, tokens], xT_lo[:, kc, tokens], w_hi[:, kc, cols], w_lo[:, kc, cols])
                        for k, (lhs, rhs) in enumerate(parts):
                            mm = nc.tensor.matmul(bank[n % 4][:], lhs, rhs, start=(kc == 0 and k == 0), stop=(kc == KC - 1 and k == 2))
                    mm.then_inc(gemm_done, 1)
                    if n == QC:
                        sum_squares(b, 0)
                    if n == QC + KVC:
                        sum_squares(b, 1)
                if not last:
                    transpose_x(b + 1)

            transpose_x(0)
            project(0)
            with pe.Fori(1, B - 1) as b:
                project(b)
            project(B - 1, last=True)

            def scores(n, u):
                A, s, i, r = UNITS * n + u, 2 * u // UNITS, u // REP % TT, u % REP
                key, tiles, _ = window(i)
                w = P * tiles
                if u % (UNITS // 2) == 0:
                    pe.wait_ge(heads_loaded[s], 3 * DMA * (n + 1))
                at_least(pe, u_ready, A - 1)
                for part in range(2):
                    mm = nc.tensor.matmul(bank[u % 2][:, 0:w], q_st[:, s, r, P * i:P * i + P],
                                          k_st[:, s, part, P * key:P * key + w], start=(part == 0), stop=(part == 1))
                mm.then_inc(s_psum, 1)

            def transpose_p(n, u):
                A, tiles = UNITS * n + u, window(u // REP % TT)[1]
                pe.wait_ge(p_ready, A + 1)
                at_least(pe, pT_ready, A - 1)
                for j in range(tiles):
                    mm = nc.tensor.transpose(bank[2 + u % 2][:, P * j:P * j + P], p_sb[:, u % RING, P * j:P * j + P], ident[:])
                mm.then_inc(pT_psum, 1)

            def weigh_values(n, u):
                A, s, r, ring = UNITS * n + u, 2 * u // UNITS, u % REP, u % RING
                key, tiles, _ = window(u // REP % TT)
                acc = bank[4 + u // REP % 2][:, 2 * HD * r:2 * HD * r + 2 * HD]
                pe.wait_ge(pT_ready, A + 1)
                if r == 0:
                    at_least(pe, o_raw_ready, 2 * TT * n + u // REP - 1)
                for j in range(tiles):
                    nc.tensor.matmul(acc, pT_hi[:, ring, P * j:P * j + P], v_st[:, s, key + j],
                                     start=(j == 0), stop=False, skip_group_check=True)
                    mm = nc.tensor.matmul(acc[:, 0:HD], pT_lo[:, ring, P * j:P * j + P], v_st[:, s, key + j, 0:HD],
                                          start=False, stop=(j == tiles - 1), skip_group_check=True)
                mm.then_inc(pv_done, 1)

            def transpose_o(t, m):
                if m == 0:
                    pe.wait_ge(tile_loaded, DMA * (t + 1))
                at_least(pe, oT_ready, 4 * t + m)
                for c in range(4):
                    mm = nc.tensor.transpose(bank[6][:, P * c:P * c + P], o_in[:, m, P * c:P * c + P], ident[:])
                mm.then_inc(oT_psum, 1)

            def project_o(t, m, products, acc):
                for j in products:
                    if j == 0:
                        pe.wait_ge(oT_ready, 4 * t + m + 1)
                    c, k = divmod(j, 3)
                    chunk = 4 * m + c
                    lhs, rhs = part_products(oT_hi[:, m % 2, c], oT_lo[:, m % 2, c], wo_hi[:, chunk], wo_lo[:, chunk])[k]
                    mm = nc.tensor.matmul(acc[:], lhs, rhs, start=(chunk == 0 and k == 0), stop=(chunk == QC - 1 and k == 2))
                    if j == 11:
                        mm.then_inc(oT_used, 1)

            def attend(n, tile=None):
                for u in range(UNITS):
                    scores(n, u)
                    for lag, work in ((2, transpose_p), (4, weigh_values)):
                        nn, uu = (n, u - lag) if u >= lag else (n - 1, UNITS + u - lag)
                        if not (isinstance(nn, int) and nn < 0):
                            work(nn, uu)
                    if tile is not None:
                        m, at = divmod(u - START, STEP)
                        if m in range(4) and at == 0:
                            transpose_o(tile, m)
                        m, at = divmod(u - START - 4, STEP)
                        if m in range(4):
                            if m == 0 and at == 0:
                                at_least(pe, y_normed, tile)
                                if isinstance(tile, int):
                                    pe.wait_ge(wo_ready, QC)
                            project_o(tile, m, (2 * at, 2 * at + 1), bank[7])

            attention_loops(pe, attend)
            for u in range(UNITS - 2, UNITS):
                transpose_p(B * TT - 1, u)
            for u in range(UNITS - 4, UNITS):
                weigh_values(B * TT - 1, u)

            def finish_tile(t, acc):
                transpose_o(t, 0)
                pe.wait_ge(y_normed, t - 1)
                for m in range(4):
                    if m < 3:
                        transpose_o(t, m + 1)
                    project_o(t, m, range(12), acc)

            pe.wait_ge(o_raw_ready, 2 * TT * B * TT)
            finish_tile(B * TT - LAG, bank[5])
            with pe.Fori(0, TT // 2) as i:
                finish_tile(B * TT - TT + 2 * i, bank[7])
                finish_tile(B * TT - TT + 1 + 2 * i, bank[5])

            def transpose_z(m):
                pe.wait_ge(z_normed, TT * m + TT)
                for kc in range(KC):
                    at_least(pe, hid_ready, IC * m if kc < 2 else IC * m - 1)
                    for i in range(TT):
                        mm = nc.tensor.transpose(bank[kc][:, P * i:P * i + P], z_in[:, i, P * kc:P * kc + P], ident[:])
                    mm.then_inc(zT_psum, 1)

            def gate_and_up(m, c):
                C = IC * m + c
                for g in range(2):
                    if c:
                        at_least(pe, hid_ready, C - 1)
                    for kc in range(KC):
                        if c == 0 and g == 0:
                            pe.wait_ge(zT_ready, KC * m + KC)
                        w = [x[:, kc, g, P * c:P * c + P] for x in (gu_hi, gu_lo)]
                        for k, (lhs, rhs) in enumerate(part_products(*w, zT_hi[:, kc], zT_lo[:, kc])):
                            mm = nc.tensor.matmul(bank[2 * (c % 2) + g][:], lhs, rhs, start=(kc == 0 and k == 0), stop=(kc == KC - 1 and k == 2))
                    mm.then_inc(gu_psum, 1)

            def down(m, c):
                pe.wait_ge(h_ready, IC * m + c + 1)
                for i in range(TT):
                    if c == 0:
                        at_least(pe, ys_ready, TT * (m - 1) + i + 1)
                    h = [x[:, c % 2, P * i:P * i + P] for x in (h_hi, h_lo)]
                    for k, (lhs, rhs) in enumerate(part_products(*h, dn_hi[:, c], dn_lo[:, c])):
                        mm = nc.tensor.matmul(bank[4 + i][:], lhs, rhs, start=(c == 0 and k == 0), stop=(c == IC - 1 and k == 2))
                mm.then_inc(down_done, 1)

            def feed_forward(m, last=False):
                for c in range(IC):
                    if isinstance(m, int) and m == 0 and c % PIECE == 0:
                        pe.wait_ge(f_ready, c + 3)
                    gate_and_up(m, c)
                    if c:
                        down(m, c - 1)
                if not last:
                    transpose_z(m + 1)
                down(m, IC - 1)

            transpose_z(0)
            feed_forward(0)
            with pe.Fori(1, B - 1) as m:
                feed_forward(m)
            feed_forward(B - 1, last=True)


def kernel(L0_attn_x, L0_attn_wq, L0_attn_wk, L0_attn_wv, L0_attn_wo, L0_attn_q_norm_w, L0_attn_k_norm_w,
           L0_ffn_gate_w, L0_ffn_up_w, L0_ffn_down_w, L0_ffn_gate_s, L0_ffn_up_s, L0_ffn_down_s):
    import concourse.bacc as bacc
    from concourse.bass_utils import run_bass_kernel_spmd

    def columns(a):
        return a.reshape(-1, P).T

    arrays = {
        "x": L0_attn_x, "wqT": np.transpose(L0_attn_wq), "wkT": np.transpose(L0_attn_wk),
        "wvT": np.transpose(L0_attn_wv), "woT": np.transpose(L0_attn_wo), "q_norm": columns(L0_attn_q_norm_w),
        "k_norm": columns(L0_attn_k_norm_w), "gateT": np.transpose(L0_ffn_gate_w), "upT": np.transpose(L0_ffn_up_w),
        "downT": np.transpose(L0_ffn_down_w), "gate_s": columns(L0_ffn_gate_s), "up_s": columns(L0_ffn_up_s), "down_s": L0_ffn_down_s,
    }
    arrays = {name: np.ascontiguousarray(a) for name, a in arrays.items()}
    nc = bacc.Bacc("TRN2", target_bir_lowering=False, num_devices=1)
    args = {name: nc.dram_tensor(name, a.shape, mybir.dt.from_np(a.dtype), kind="ExternalInput").ap() for name, a in arrays.items()}
    out = nc.dram_tensor("out", (B, T, D), F32, kind="ExternalOutput").ap()
    sandwich_layer(nc, **args, out=out)
    result = run_bass_kernel_spmd(nc, [arrays], core_ids=[0])
    return result.results[0]["out"]
```

```python
from contextlib import ExitStack

import concourse.bass as bass
import numpy as np
from concourse import mybir

F32 = mybir.dt.float32
F32R = mybir.dt.float32r
F16 = mybir.dt.float16
ACT = mybir.ActivationFunctionType
ALU = mybir.AluOpType

P = 128
B, T, D = 4, 512, 512
H, G, HD = 32, 8, 64
REP = H // G
WINDOW = 256
INTER = 1408
KC = D // P
TT = T // P
QC, KVC = H * HD // P, G * HD // P
WQKV = (H + 2 * G) * HD
NB = WINDOW // P + 1
WIN = NB * P
IC = INTER // P
RMS_EPS, LN_EPS = 1e-6, 1e-5
BIG = 1e30
VSCALE = 1024.0
NGEMM = QC + KVC + TT
NSQ = QC + KVC - 2
QK_RING = 4
LATE = 7
WBLOCKS = WQKV // T
UNITS = 2 * TT * REP
LAG = TT + 1
STEP = 6
START = 2
RING = 4
PIECE = 3
DMA = 16
RATIO = 2.0 ** (-8.0 / H)
TINY = 1e-30
CONSTANTS = 6


def projection_schedule():
    order, norms, late = [], iter(range(LATE)), iter(range(LATE, QC + KVC))
    for n in range(NGEMM):
        order.append(("gemm", n))
        order += [("late norm", f) for _, f in zip(range(2), late)]
        if n == QC + 1:
            order.append(("root", 0))
        if n > QC:
            order += [("norm", f) for _, f in zip(range(1), norms)]
        if n == QC + KVC + 1:
            order.append(("root", 1))
    return order


def feed_forward_pieces():
    return [(kind, c, min(PIECE, IC - c)) for c in range(0, IC, PIECE) for kind in ("gate", "up", "down")]


SCHEDULE = projection_schedule()
PIECES = feed_forward_pieces()


def attention_loops(eng, attend):
    attend(0)
    with eng.Fori(1, LAG) as n:
        attend(n)
    attend(LAG, 0)
    with eng.Fori(1, TT) as i:
        attend(LAG + i, i)
    with eng.Fori(0, TT) as i:
        attend(LAG + TT + i, TT + i)
    with eng.Fori(0, TT - 1) as i:
        attend(LAG + 2 * TT + i, 2 * TT + i)


def at_least(eng, sem, value):
    if isinstance(value, int) and value <= 0:
        return
    eng.wait_ge(sem, value)


def part_products(a_hi, a_lo, b_hi, b_lo):
    return ((a_hi, b_hi), (a_lo, b_hi), (a_hi, b_lo))


def window(i):
    first = max(0, i - NB + 1)
    return first, i - first + 1, (first - i + NB - 1) * P


def qk_stores(b, f):
    return DMA * ((QC + KVC) // QK_RING * b + f // QK_RING)


def sandwich_layer(nc, x, wqT, wkT, wvT, woT, q_norm, k_norm, gateT, upT, downT, gate_s, up_s, down_s, out):
    x_t = x.rearrange("b (i p) d -> b p i d", p=P)
    out_t = out.rearrange("b (i p) d -> b p i d", p=P)
    x_flat = x.rearrange("b (i p) d -> (b i) p d", p=P)

    q_scr = nc.dram_tensor("q_scr", [B * H, HD, 2, T], F32, kind="Internal").ap()
    k_scr = nc.dram_tensor("k_scr", [B * G, HD, 2, T], F32, kind="Internal").ap()
    v_scr = nc.dram_tensor("v_scr", [B * G, P, TT, 2 * HD], F16, kind="Internal").ap()
    o_scr = nc.dram_tensor("o_scr", [B * TT, TT, P, 2 * REP * HD], F32, kind="Internal").ap()
    vn_scr = nc.dram_tensor("vn_scr", [P, G * HD], F32, kind="Internal").ap()
    z_scr = nc.dram_tensor("z_scr", [B * TT, P, D], F32, kind="Internal").ap()

    with ExitStack() as ctx:
        def sb(scope, name, shape, dt=F32):
            return scope.enter_context(nc.sbuf_tensor(name, shape, dt))

        def sem(name):
            return ctx.enter_context(nc.semaphore(name))

        def sems(names):
            return [sem(name) for name in names.split()]

        bank = [ctx.enter_context(nc.psum_tensor(f"bank{i}", [P, 512], F32)) for i in range(8)]

        ident = sb(ctx, "ident", [P, P])
        ones = sb(ctx, "ones", [P, P])
        stats = sb(ctx, "stats", [P, TT, 6])
        moments = sb(ctx, "moments", [P, TT, 2])
        var_eps = sb(ctx, "var_eps", [P, TT])
        rstd = sb(ctx, "rstd", [P, TT])
        minus_half = sb(ctx, "minus_half", [P, TT])
        eps_rms = sb(ctx, "eps_rms", [P, 1])
        eps_tiny = sb(ctx, "eps_tiny", [P, 1])
        warm = sb(ctx, "warm", [P, 1])

        dist = sb(ctx, "dist", [P, WIN])
        slopes = sb(ctx, "slopes", [P, H + 4 * REP])

        early = ctx.enter_context(ExitStack())
        bias = sb(early, "bias", [P, 2, REP, WIN])
        with ExitStack() as s1:
            w_hi = sb(s1, "w_hi", [P, WBLOCKS, KC, T], F32R)
            w_lo = sb(s1, "w_lo", [P, WBLOCKS, KC, T], F32R)
            xT_hi = sb(s1, "xT_hi", [P, KC, T], F32R)
            xT_lo = sb(s1, "xT_lo", [P, KC, T], F32R)
            x_in = sb(s1, "x_in", [P, TT, D])
            raw = sb(s1, "raw", [P, QC + KVC, T])
            square = sb(s1, "square", [P, 2, T])
            sum_sq = sb(s1, "sum_sq", [P, 2, T])
            inv_rms = sb(s1, "inv_rms", [P, 2, T])
            v_out = sb(s1, "v_out", [P, 2, G, 2, HD], F16)
            qn_raw = sb(s1, "qn_raw", [P, QC])
            norm_w = sb(s1, "norm_w", [P, QC + KVC])
            with ExitStack() as before_norms:
                w_stage = sb(before_norms, "w_stage", [P, 2, KC, T])
            qk = sb(s1, "qk", [P, QK_RING, 2, T], F32R)

        with ExitStack() as s2:
            q_st = sb(s2, "q_st", [P, 2, REP, T], F32R)
            k_st = sb(s2, "k_st", [P, 2, 2, T], F32R)
            v_st = sb(s2, "v_st", [P, 2, TT, 2 * HD], F16)
            wo_hi = sb(s2, "wo_hi", [P, QC, D], F32R)
            wo_lo = sb(s2, "wo_lo", [P, QC, D], F32R)
            v_norm = sb(s2, "v_norm", [P, G + 2, HD])
            u_sb = sb(s2, "u_sb", [P, RING, WIN])
            low = sb(s2, "low", [P, RING])
            p_sb = sb(s2, "p_sb", [P, RING, WIN])
            pT_hi = sb(s2, "pT_hi", [P, RING, WIN], F16)
            pT_lo = sb(s2, "pT_lo", [P, RING, WIN], F16)
            p_sum = sb(s2, "p_sum", [P, TT, REP])
            inv_sum = sb(s2, "inv_sum", [P, 2, REP])
            o_low = sb(s2, "o_low", [P, REP, HD])
            o_raw = sb(s2, "o_raw", [P, 2, REP, HD])
            o_mid = sb(s2, "o_mid", [P, REP, HD])
            o_out = sb(s2, "o_out", [P, 2, REP, HD])
            wo_stage = sb(s2, "wo_stage", [P, TT, D])
            o_in = sb(s2, "o_in", [P, TT, 2 * REP * HD])
            oT_hi = sb(s2, "oT_hi", [P, 2, 4, P], F32R)
            oT_lo = sb(s2, "oT_lo", [P, 2, 4, P], F32R)
            x_res = sb(s2, "x_res", [P, D])
            y_n = sb(s2, "y_n", [P, D])
            z_out = sb(s2, "z_out", [P, D])

        early.close()

        with ExitStack() as s4:
            gu_hi = sb(s4, "gu_hi", [P, KC, 2, INTER], F32R)
            gu_lo = sb(s4, "gu_lo", [P, KC, 2, INTER], F32R)
            dn_hi = sb(s4, "dn_hi", [P, IC, D], F32R)
            dn_lo = sb(s4, "dn_lo", [P, IC, D], F32R)
            f_stage = sb(s4, "f_stage", [P, 2, KC * PIECE * P])
            zT_hi = sb(s4, "zT_hi", [P, KC, T], F32R)
            zT_lo = sb(s4, "zT_lo", [P, KC, T], F32R)
            z_in = sb(s4, "z_in", [P, TT, D])
            silu = sb(s4, "silu", [P, T])
            hid = sb(s4, "hid", [P, T])
            h_hi = sb(s4, "h_hi", [P, 2, T], F32R)
            h_lo = sb(s4, "h_lo", [P, 2, T], F32R)
            y_s = sb(s4, "y_s", [P, TT, D])
            z_res = sb(s4, "z_res", [P, TT, D])
            gate_sc = sb(s4, "gate_sc", [P, IC])
            up_sc = sb(s4, "up_sc", [P, IC])
            down_sc = sb(s4, "down_sc", [P, D])

        const_ready, x_loaded, norm_loaded, norm_ready, vn_stored = sems(
            "const_ready x_loaded norm_loaded norm_ready vn_stored")
        w_loaded = sems("w_loaded0 w_loaded1")
        w_hi_ready, w_ready, v_squared, v_norm_psum, v_norm_ready, v_inv_ready, v_scaled = sems(
            "w_hi_ready w_ready v_squared v_norm_psum v_norm_ready v_inv_ready v_scaled")
        ln_stats, ln_moments, ln_var, ln_rstd, ln_done = sems("ln_stats ln_moments ln_var ln_rstd ln_done")
        xT_psum, xT_hi_ready, xT_ready, gemm_done = sems("xT_psum xT_hi_ready xT_ready gemm_done")
        raw_ready, sq_ready, acc_ready, ssq_psum, root_ready, inv_ready = sems(
            "raw_ready sq_ready acc_ready ssq_psum root_ready inv_ready")
        scaled, qk_hi_ready, qk_ready, v_hi_ready, v_ready = sems("scaled qk_hi_ready qk_ready v_hi_ready v_ready")
        qk_stored, v_stored = sems("qk_stored0 qk_stored1 qk_stored2 qk_stored3"), sems("v_stored0 v_stored1")
        held = sem("held")
        heads_loaded, o_stored, wo_loaded = sems("heads_loaded0 heads_loaded1"), sems("o_stored0 o_stored1"), sem("wo_loaded")
        dist_ready, bias_ready, vn_loaded = sems("dist_ready bias_ready vn_loaded")
        s_psum, u_ready, p_ready, pT_psum, pT_hi_ready, pT_ready, pv_done = sems(
            "s_psum u_ready p_ready pT_psum pT_hi_ready pT_ready pv_done")
        inv_sum_ready, o_low_ready, o_raw_ready, o_mid_ready, o_ready = sems(
            "inv_sum_ready o_low_ready o_raw_ready o_mid_ready o_ready")
        wo_hi_ready, wo_ready, tile_loaded, res1_loaded, oT_psum, oT_hi_ready, oT_ready, oT_used = sems(
            "wo_hi_ready wo_ready tile_loaded res1_loaded oT_psum oT_hi_ready oT_ready oT_used")
        y_stats, y_moments, y_var, y_rstd, y_normed, z_ready, z_stored = sems(
            "y_stats y_moments y_var y_rstd y_normed z_ready z_stored")
        f_loaded = sems("f_loaded0 f_loaded1")
        f_hi_ready, f_ready, scales_loaded, z_loaded, z_stats, z_moments, z_var, z_rstd, z_normed = sems(
            "f_hi_ready f_ready scales_loaded z_loaded z_stats z_moments z_var z_rstd z_normed")
        zT_psum, zT_hi_ready, zT_ready, gu_psum, silu_ready, hid_ready, h_hi_ready, h_ready = sems(
            "zT_psum zT_hi_ready zT_ready gu_psum silu_ready hid_ready h_hi_ready h_ready")
        down_done, ys_ready, f_stats, f_moments, f_var, f_rstd, f_normed, f_sum, res_loaded, out_stored = sems(
            "down_done ys_ready f_stats f_moments f_var f_rstd f_normed f_sum res_loaded out_stored")

        def piece(j):
            kind, at, size = PIECES[j]
            if kind == "down":
                src = f_stage[:, j % 2, 0:size * D].rearrange("p (c d) -> p c d", c=size)
                return src, dn_hi[:, at:at + size], dn_lo[:, at:at + size]
            src = f_stage[:, j % 2, 0:KC * P * size].rearrange("p (k n) -> p k n", k=KC)
            g = ("gate", "up").index(kind)
            return (src, *(w[:, :, g, P * at:P * (at + size)] for w in (gu_hi, gu_lo)))

        block = ctx.enter_context(nc.Block())

        def hold(eng):
            eng.sem_inc(held, 1)

        @block.sync
        def _(sp):
            w_src = [wqT[:, T * j:T * j + T] for j in range(H * HD // T)] + [wkT, wvT]

            def load_weights(j):
                at_least(sp, w_ready, j - 1)
                sp.dma_start(w_stage[:, j % 2], w_src[j].rearrange("(k p) n -> p k n", p=P)).then_inc(w_loaded[j % 2], DMA)

            sp.dma_start(x_in[:], x_t[0]).then_inc(x_loaded, DMA)
            load_weights(0)
            sp.dma_start(qn_raw[:], q_norm).then_inc(norm_loaded, DMA)
            sp.dma_start(norm_w[:, QC:], k_norm).then_inc(norm_loaded, DMA)
            for j in range(1, WBLOCKS):
                load_weights(j)

            def project(b, last=False):
                if not last:
                    sp.wait_ge(xT_psum, KC * b + KC)
                    sp.dma_start(x_in[:], x_t[bass.ds(b + 1, 1)].rearrange("a p i d -> p (a i) d")).then_inc(x_loaded, DMA)
                for kind, n in SCHEDULE:
                    if kind == "gemm" and n == QC + 1 and isinstance(b, int) and b == 0:
                        sp.wait_ge(v_norm_ready, 1)
                        sp.dma_start(vn_scr, raw[:, QC + KVC - 1]).then_inc(vn_stored, DMA)
                    if kind == "gemm" and n >= QC + KVC:
                        i = n - QC - KVC
                        sp.wait_ge(v_ready, TT * b + i + 1)
                        sp.dma_start(v_scr[bass.ds(b * G, G), :, i].rearrange("g p n -> p g n"),
                                     v_out[:, i % 2].rearrange("p g t d -> p g (t d)")).then_inc(v_stored[i % 2], DMA)
                    if kind == "root" and n == 0 and last:
                        stage1_stored(b)
                        sp.wait_ge(vn_stored, DMA)
                        sp.wait_ge(gemm_done, NGEMM * b + QC)
                        load_heads(0, 0)
                        load_heads(0, 1)
                    if kind == "norm":
                        store_qk(b, n)
                    if kind == "late norm" and not (isinstance(b, int) and b == 0):
                        store_qk(b - 1, n)

            def store_qk(b, f):
                sp.wait_ge(qk_ready, (QC + KVC) * b + f + 1)
                scr, head = (q_scr, b * H + 2 * f) if f < QC else (k_scr, b * G + 2 * (f - QC))
                sp.dma_start(scr[bass.ds(head, 2)].rearrange("h d t n -> (h d) t n"),
                             qk[:, f % QK_RING].bitcast(F32)).then_inc(qk_stored[f % QK_RING], DMA)

            def stage1_stored(batches):
                for s in range(QK_RING):
                    sp.wait_ge(qk_stored[s], qk_stores(batches, 0))
                for s in range(2):
                    sp.wait_ge(v_stored[s], DMA * batches * TT // 2)

            def load_heads(n, s):
                at_least(sp, pv_done, UNITS * (n - 1) + UNITS // 2 * (s + 1))
                g = 2 * n + s
                for copy in range(2):
                    sp.dma_start(k_st[copy:P:2, s].bitcast(F32),
                                 k_scr[bass.ds(g, 1)].rearrange("a d t n -> (a d) t n")).then_inc(heads_loaded[s], DMA)
                sp.dma_start(q_st[:, s].bitcast(F32),
                             q_scr[bass.ds(g * REP, REP)].rearrange("h d t n -> (d t) h n")).then_inc(heads_loaded[s], DMA)
                sp.dma_start(v_st[:, s],
                             v_scr[bass.ds(g, 1)].rearrange("a p i n -> (a p) i n")).then_inc(heads_loaded[s], DMA)

            project(0)
            with sp.Fori(1, B - 1) as b:
                project(b)
            project(B - 1, last=True)

            def store_o(n, s, tiles):
                for i in tiles:
                    sp.wait_ge(o_ready, 2 * TT * n + TT * s + i + 1)
                    sp.dma_start(o_scr[bass.ds(n, 1), i, :, s * REP * HD:(s + 1) * REP * HD].rearrange("a p c -> (a p) c"),
                                 o_out[:, i % 2].rearrange("p r d -> p (r d)")).then_inc(o_stored[i % 2], DMA)

            def load_o(b, i):
                at_least(sp, oT_psum, 4 * (TT * b + i))
                sp.dma_start(o_in[:], o_scr[bass.ds(b * TT, TT), bass.ds(i, 1)].rearrange("g a p c -> p (g a) c")).then_inc(tile_loaded, DMA)

            def load_residual(t):
                at_least(sp, z_ready, t)
                sp.dma_start(x_res[:], x_flat[bass.ds(t, 1)].rearrange("a p d -> (a p) d")).then_inc(res1_loaded, DMA)

            def store_z(t):
                sp.wait_ge(z_ready, t + 1)
                sp.dma_start(z_scr[bass.ds(t, 1)].rearrange("a p d -> (a p) d"), z_out[:]).then_inc(z_stored, DMA)

            def load_wo(group):
                at_least(sp, wo_ready, TT * group)
                sp.dma_start(wo_stage[:], woT.rearrange("(g c p) d -> g p c d", g=QC // TT, p=P)[bass.ds(group, 1)]
                             .rearrange("a p c d -> p (a c) d")).then_inc(wo_loaded, DMA)

            def attend(n, tile=None, wo=False):
                load_heads(n, 0)
                if tile is not None:
                    for k in range(2):
                        sp.wait_ge(o_stored[k], DMA * (4 * (n - 1) + 2 - k))
                    hold(sp)
                    load_o(*tile)
                store_o(n - 1, 0, [TT - 1])
                store_o(n - 1, 1, range(TT - 1))
                load_heads(n, 1)
                store_o(n - 1, 1, [TT - 1])
                store_o(n, 0, [0])
                if tile is not None:
                    t = TT * tile[0] + tile[1]
                    if not isinstance(t, int):
                        store_z(t - 1)
                    load_residual(t)
                store_o(n, 0, range(1, TT - 1))
                if wo:
                    load_wo(n)

            sp.wait_ge(gemm_done, NGEMM * B)
            sp.dma_start(v_norm[:, 0:G].rearrange("p g d -> p (g d)"), vn_scr).then_inc(vn_loaded, DMA)
            sp.dma_start(v_norm[:, G:G + 2].rearrange("p g d -> p (g d)"), vn_scr[:, 0:2 * HD]).then_inc(vn_loaded, DMA)
            for f in range(LATE, QC + KVC):
                store_qk(B - 1, f)
            stage1_stored(B)
            load_wo(0)
            store_o(0, 0, range(TT - 1))
            with sp.Fori(1, LAG - 1) as n:
                attend(n, wo=True)
            attend(LAG - 1)
            attend(LAG, (0, 0))
            with sp.Fori(1, TT) as i:
                attend(LAG + i, (0, i))
            with sp.Fori(0, TT) as i:
                attend(LAG + TT + i, (1, i))
            with sp.Fori(0, TT - 1) as i:
                attend(LAG + 2 * TT + i, (2, i))
            store_o(B * TT - 1, 0, [TT - 1])
            store_o(B * TT - 1, 1, range(TT))
            for k in range(2):
                sp.wait_ge(o_stored[k], DMA * 4 * B * TT)
            load_o(B - 2, TT - 1)
            with sp.Fori(0, TT) as i:
                store_z(TT * (B - 1) + i - 2)
                load_residual(TT * (B - 1) + i - 1)
                load_o(B - 1, i)
            store_z(B * TT - 2)
            load_residual(B * TT - 1)
            store_z(B * TT - 1)
            sp.wait_ge(z_stored, DMA * B * TT)

            def load_z(tile, m, done):
                sp.dma_start(tile[:], z_scr[bass.ds(TT * m, TT)].rearrange("i p d -> p i d")).then_inc(done, DMA)

            load_z(z_in, 0, z_loaded)
            sp.dma_start(gate_sc[:], gate_s).then_inc(scales_loaded, DMA)
            sp.dma_start(up_sc[:], up_s).then_inc(scales_loaded, DMA)
            sp.dma_start(down_sc[:], down_s.partition_broadcast(P)).then_inc(scales_loaded, DMA)
            for j, (kind, at, size) in enumerate(PIECES):
                at_least(sp, f_ready, j - 1)
                if kind == "down":
                    src = downT[P * at:P * (at + size), :].rearrange("(c p) d -> p c d", p=P)
                    dst = f_stage[:, j % 2, 0:size * D].rearrange("p (c d) -> p c d", c=size)
                else:
                    src = (gateT if kind == "gate" else upT)[:, P * at:P * (at + size)].rearrange("(k p) n -> p k n", p=P)
                    dst = f_stage[:, j % 2, 0:KC * P * size].rearrange("p (k n) -> p k n", k=KC)
                sp.dma_start(dst, src).then_inc(f_loaded[j % 2], DMA)

            def feed_forward(m, last=False):
                if not last:
                    sp.wait_ge(zT_psum, KC * m + KC)
                    load_z(z_in, m + 1, z_loaded)
                at_least(sp, f_sum, TT * m)
                load_z(z_res, m, res_loaded)
                sp.wait_ge(f_sum, TT * m + TT)
                sp.dma_start(out_t[bass.ds(m, 1)].rearrange("a p i d -> p (a i) d"), y_s[:]).then_inc(out_stored, DMA)

            feed_forward(0)
            with sp.Fori(1, B - 1) as m:
                feed_forward(m)
            feed_forward(B - 1, last=True)
            sp.wait_ge(out_stored, DMA * B)

        @block.gpsimd
        def _(pool):
            nc.gpsimd.memset(ident[:], 0.0).then_inc(const_ready, 1)
            nc.gpsimd.memset(ones[:], 1.0).then_inc(const_ready, 1)
            nc.gpsimd.memset(minus_half[:], -0.5).then_inc(const_ready, 1)
            nc.gpsimd.memset(eps_rms[:], RMS_EPS).then_inc(const_ready, 1)
            nc.gpsimd.memset(eps_tiny[:], TINY).then_inc(const_ready, 1)
            pool.wait_ge(const_ready, 5)
            nc.gpsimd.affine_select(out=ident[:], in_=ident[:], compare_op=ALU.not_equal, fill=1.0, base=0,
                                    pattern=[[-1, P]], channel_multiplier=1).then_inc(const_ready, 1)

            def inverse_root(count, var_ready, value, done):
                pool.wait_ge(var_ready, value)
                nc.gpsimd.tensor_tensor(out=rstd[:, 0:count], in0=var_eps[:, 0:count], in1=minus_half[:, 0:count],
                                        op=ALU.pow).then_inc(done, 1)

            inverse_root(TT, ln_var, 1, ln_rstd)

            nc.gpsimd.iota(dist[:], pattern=[[-1, WIN]], base=WINDOW, channel_multiplier=1,
                           allow_small_or_imprecise_dtypes=True).then_inc(dist_ready, 1)
            for h in range(H + 4 * REP):
                nc.gpsimd.memset(slopes[:, h:h + 1], float(np.float32(RATIO ** (h % H)))).then_inc(dist_ready, 1)
            pool.wait_ge(dist_ready, 1 + H + 4 * REP)
            nc.gpsimd.affine_select(out=dist[:], in_=dist[:], compare_op=ALU.is_ge, fill=BIG, base=WINDOW,
                                    pattern=[[-1, WIN]], channel_multiplier=1).then_inc(dist_ready, 1)
            pool.wait_ge(dist_ready, 2 + H + 4 * REP)
            nc.gpsimd.affine_select(out=dist[:], in_=dist[:], compare_op=ALU.is_ge, fill=BIG, base=0,
                                    pattern=[[1, WIN]], channel_multiplier=-1).then_inc(dist_ready, 1)
            pool.wait_ge(dist_ready, 3 + H + 4 * REP)

            with pool.Fori(1, B) as b:
                inverse_root(TT, ln_var, b + 1, ln_rstd)

            def make_bias(n, q, s):
                at_least(pool, u_ready, UNITS * (n - 1) + UNITS // 2 * (s + 1))
                hold(pool)
                nc.gpsimd.tensor_tensor(out=bias[:, s], in0=dist[:].unsqueeze(1).broadcast_to([P, REP, WIN]),
                                        in1=slopes[:, bass.ds(2 * REP * q + REP * s, REP)].unsqueeze(2).broadcast_to([P, REP, WIN]),
                                        op=ALU.mult).then_inc(bias_ready, 1)

            def finish_o(n, q, s, i):
                a = 2 * TT * n + TT * s + i
                pool.wait_ge(inv_sum_ready, a + 1)
                pool.wait_ge(o_raw_ready, a + 1)
                at_least(pool, o_ready, a)
                nc.gpsimd.tensor_tensor(out=o_mid[:], in0=o_raw[:, i % 2],
                                        in1=inv_sum[:, i % 2].unsqueeze(2).broadcast_to([P, REP, HD]),
                                        op=ALU.mult).then_inc(o_mid_ready, 1)
                pool.wait_ge(o_mid_ready, a + 1)
                at_least(pool, o_stored[i % 2], DMA * (TT * n + TT // 2 * s + i // 2))
                hold(pool)
                nc.gpsimd.tensor_tensor(out=o_out[:, i % 2], in0=o_mid[:],
                                        in1=v_norm[:, bass.ds(2 * q + s, 1)].broadcast_to([P, REP, HD]),
                                        op=ALU.mult).then_inc(o_ready, 1)

            def split_wo(group, i):
                chunk = bass.ds(TT * group + i, 1)
                pool.wait_ge(wo_loaded, DMA * (group + 1))
                hold(pool)
                nc.gpsimd.tensor_copy(wo_hi[:, chunk], wo_stage[:, i:i + 1]).then_inc(wo_hi_ready, 1)
                pool.wait_ge(wo_hi_ready, TT * group + i + 1)
                hold(pool)
                nc.gpsimd.tensor_tensor(out=wo_lo[:, chunk], in0=wo_stage[:, i:i + 1], in1=wo_hi[:, chunk].bitcast(F32),
                                        op=ALU.subtract).then_inc(wo_ready, 1)

            def add_residual(t):
                pool.wait_ge(y_normed, t + 1)
                pool.wait_ge(res1_loaded, DMA * (t + 1))
                at_least(pool, z_stored, DMA * t)
                nc.gpsimd.tensor_tensor(out=z_out[:], in0=y_n[:], in1=x_res[:], op=ALU.add).then_inc(z_ready, 1)

            def attend(n, q, tile=None, wo=False):
                for i in range(TT // 2, TT):
                    finish_o(n - 1, q - 1, 1, i)
                make_bias(n, q, 1)
                for i in range(TT):
                    finish_o(n, q, 0, i)
                    if wo:
                        split_wo(n - 1, i)
                    if i == 0 and tile is not None and not (isinstance(tile, int) and tile == 0):
                        add_residual(tile - 1)
                make_bias(n + 1, q + 1, 0)
                for i in range(TT // 2):
                    finish_o(n, q, 1, i)
                if tile is not None:
                    inverse_root(1, y_var, tile + 1, y_rstd)

            make_bias(0, 0, 0)
            make_bias(0, 0, 1)
            pool.wait_ge(vn_loaded, 2 * DMA)
            for i in range(TT):
                finish_o(0, 0, 0, i)
            make_bias(1, 1, 0)
            for i in range(TT // 2):
                finish_o(0, 0, 1, i)
            with pool.Fori(1, LAG) as n:
                attend(n, n, wo=True)
            attend(LAG, 1, 0)
            with pool.Fori(1, TT) as i:
                attend(LAG + i, i + 1, i)
            with pool.Fori(0, TT) as i:
                attend(LAG + TT + i, i + 1, TT + i)
            with pool.Fori(0, TT - 1) as i:
                attend(LAG + 2 * TT + i, i + 1, 2 * TT + i)
            for i in range(TT // 2, TT):
                finish_o(B * TT - 1, TT - 1, 1, i)
            add_residual(B * TT - LAG - 1)
            with pool.Fori(B * TT - LAG, B * TT) as t:
                inverse_root(1, y_var, t + 1, y_rstd)
                add_residual(t)

            inverse_root(TT, z_var, 1, z_rstd)

            def feed_forward(m, last=False):
                if not last:
                    inverse_root(TT, z_var, m + 2, z_rstd)
                inverse_root(TT, f_var, m + 1, f_rstd)
                pool.wait_ge(res_loaded, DMA * (m + 1))
                for i in range(TT):
                    pool.wait_ge(f_normed, TT * m + i + 1)
                    nc.gpsimd.tensor_tensor(out=y_s[:, i], in0=y_s[:, i], in1=z_res[:, i], op=ALU.add).then_inc(f_sum, 1)

            with pool.Fori(0, B - 1) as m:
                feed_forward(m)
            feed_forward(B - 1, last=True)

        @block.scalar
        def _(act):
            act.wait_ge(const_ready, CONSTANTS)
            nc.scalar.activation(warm[:], ones[:, 0:1], ACT.Sqrt)

            def round_xT(b):
                at_least(act, gemm_done, NGEMM * b)
                for kc in range(KC):
                    act.wait_ge(xT_psum, KC * b + kc + 1)
                    nc.scalar.activation(xT_hi[:, kc], bank[4 + kc][:], ACT.Copy).then_inc(xT_hi_ready, 1)

            def square_v():
                act.wait_ge(w_loaded[1], DMA * WBLOCKS // 2)
                for kc in range(KC):
                    nc.scalar.activation(raw[:, QC + kc], w_stage[:, 1, kc], ACT.Square).then_inc(v_squared, 1)

            def norm_of_v():
                act.wait_ge(v_norm_psum, 1)
                nc.scalar.activation(raw[:, QC + KVC - 1], bank[7][:], ACT.Sqrt, scale=VSCALE ** -2,
                                     bias=eps_tiny[:]).then_inc(v_norm_ready, 1)

            def norm(b, f):
                act.wait_ge(scaled, (QC + KVC) * b + f + 1)
                at_least(act, qk_stored[f % QK_RING], qk_stores(b, f))
                nc.scalar.activation(qk[:, f % QK_RING, 0], raw[:, f], ACT.Copy).then_inc(qk_hi_ready, 1)

            def project(b, last=False):
                first = isinstance(b, int) and b == 0
                for kind, n in SCHEDULE:
                    if kind == "norm":
                        norm(b, n)
                    elif kind == "late norm":
                        if not first:
                            norm(b - 1, n)
                    elif kind == "root":
                        act.wait_ge(ssq_psum, 2 * b + n + 1)
                        if first and n == 1:
                            act.wait_ge(v_scaled, 1)
                        nc.scalar.activation(inv_rms[:, n], bank[6 + n][:], ACT.Sqrt, scale=1.0 / (D if n else H * HD),
                                             bias=eps_rms[:]).then_inc(root_ready, 1)
                    elif kind == "gemm" and n < QC + KVC:
                        if first and n == QC - 1:
                            square_v()
                        if first and n == QC:
                            norm_of_v()
                        if first and n == QC + KVC - 1:
                            act.wait_ge(vn_stored, DMA)
                            act.wait_ge(v_inv_ready, 1)
                        act.wait_ge(gemm_done, NGEMM * b + n + 1)
                        at_least(act, qk_ready, (QC + KVC) * (b - 1) + n + 1)
                        nc.scalar.activation(raw[:, n], bank[n % 4][:], ACT.Copy).then_inc(raw_ready, 1)
                        if n in (0, QC):
                            at_least(act, ssq_psum, 2 * (b - 1) + n // QC + 1)
                            dst = sum_sq[:, n // QC]
                        else:
                            m = n - 1 - n // QC
                            at_least(act, acc_ready, NSQ * b + m - 1)
                            dst = square[:, m % 2]
                        nc.scalar.activation(dst, bank[n % 4][:], ACT.Square).then_inc(sq_ready, 1)
                    elif kind == "gemm":
                        i = n - QC - KVC
                        if n == NGEMM - 1 and not last:
                            round_xT(b + 1)
                        act.wait_ge(gemm_done, NGEMM * b + n + 1)
                        at_least(act, v_stored[i % 2], DMA * (TT // 2 * b + i // 2))
                        nc.scalar.activation(v_out[:, i % 2, :, 0], bank[n % 4][:].rearrange("p (g d) -> p g d", g=G),
                                             ACT.Copy).then_inc(v_hi_ready, 1)

            round_xT(0)
            project(0)
            with act.Fori(1, B - 1) as b:
                project(b)
            project(B - 1, last=True)

            nc.scalar.activation(warm[:], ones[:, 0:1], ACT.Exp)

            def exps(n, u):
                A, i, r = UNITS * n + u, u // REP % TT, u % REP
                a, w = 2 * TT * n + u // REP, P * window(i)[1]
                act.wait_ge(u_ready, A + 1)
                at_least(act, pT_psum, A - RING + 1)
                if r == 0:
                    at_least(act, inv_sum_ready, a - TT + 1)
                nc.scalar.activation(p_sb[:, u % RING, 0:w], u_sb[:, u % RING, 0:w], ACT.Exp, scale=-1.0,
                                     bias=low[:, u % RING:u % RING + 1],
                                     accum_out=p_sum[:, i, r:r + 1]).then_inc(p_ready, 1)

            def round_pT(n, u):
                A, w = UNITS * n + u, P * window(u // REP % TT)[1]
                act.wait_ge(pT_psum, A + 1)
                at_least(act, pv_done, A - RING + 1)
                nc.scalar.activation(pT_hi[:, u % RING, 0:w], bank[2 + u % 2][:, 0:w], ACT.Copy).then_inc(pT_hi_ready, 1)

            def copy_low(n, u):
                act.wait_ge(pv_done, UNITS * n + u + 1)
                at_least(act, o_raw_ready, 2 * TT * n + u // REP)
                nc.scalar.activation(o_low[:], bank[4 + u // REP % 2][:].rearrange("p (r t d) -> p r t d", r=REP, t=2)[:, :, 1],
                                     ACT.Copy).then_inc(o_low_ready, 1)

            def round_oT(t, m):
                act.wait_ge(oT_psum, 4 * t + m + 1)
                at_least(act, oT_used, 4 * t + m - 1)
                nc.scalar.activation(oT_hi[:, m % 2].rearrange("p c n -> p (c n)"), bank[6][:], ACT.Copy).then_inc(oT_hi_ready, 1)

            def attend(n, tile=None):
                for u in range(UNITS):
                    for lag, work in ((2, round_pT), (0, exps), (5, copy_low)):
                        nn, uu = (n, u - lag) if u >= lag else (n - 1, UNITS + u - lag)
                        if not (isinstance(nn, int) and nn < 0) and (work is not copy_low or uu % REP == REP - 1):
                            work(nn, uu)
                    if isinstance(n, int) and n == 0 and u + LATE < QC + KVC:
                        norm(B - 1, u + LATE)
                    m, at = divmod(u - START - 1, STEP)
                    if tile is not None and m in range(4) and at == 0:
                        round_oT(tile, m)

            attention_loops(act, attend)
            round_pT(B * TT - 1, UNITS - 2)
            copy_low(B * TT - 1, UNITS - 1 - REP)
            round_pT(B * TT - 1, UNITS - 1)
            copy_low(B * TT - 1, UNITS - 1)

            with act.Fori(B * TT - LAG, B * TT) as t:
                for m in range(4):
                    round_oT(t, m)

            nc.scalar.activation(warm[:], ones[:, 0:1], ACT.Silu)

            def round_zT(m):
                for kc in range(KC):
                    act.wait_ge(zT_psum, KC * m + kc + 1)
                    nc.scalar.activation(zT_hi[:, kc], bank[kc][:], ACT.Copy).then_inc(zT_hi_ready, 1)

            def feed_forward(m, last=False):
                for c in range(IC):
                    C = IC * m + c
                    if isinstance(m, int) and m == 0 and c % PIECE == 0:
                        for j in range(c, c + 3):
                            kind, at, size = PIECES[j]
                            act.wait_ge(f_loaded[j % 2], DMA * (j // 2 + 1))
                            src, hi, _ = piece(j)
                            nc.scalar.activation(hi, src, ACT.Copy).then_inc(f_hi_ready, 1)
                    if isinstance(m, int) and m == 0 and c == 0:
                        act.wait_ge(scales_loaded, 3 * DMA)
                    act.wait_ge(gu_psum, 2 * C + 1)
                    at_least(act, hid_ready, C)
                    nc.scalar.activation(silu[:], bank[2 * (c % 2)][:], ACT.Silu, scale=gate_sc[:, c:c + 1]).then_inc(silu_ready, 1)
                    act.wait_ge(hid_ready, C + 1)
                    at_least(act, down_done, C - 1 + (c == 0))
                    nc.scalar.activation(h_hi[:, c % 2], hid[:], ACT.Copy).then_inc(h_hi_ready, 1)
                if not last:
                    round_zT(m + 1)

            round_zT(0)
            feed_forward(0)
            with act.Fori(1, B - 1) as m:
                feed_forward(m)
            feed_forward(B - 1, last=True)

        @block.vector
        def _(dve):
            def layer_stats(k, loaded, value, tiles, stats_ready, moments_ready, var_ready):
                count = len(tiles)
                dve.wait_ge(loaded, value)
                for i, tile in enumerate(tiles):
                    nc.vector.bn_stats(stats[:, i], tile).then_inc(stats_ready, 1)
                for i in range(count):
                    dve.wait_ge(stats_ready, count * k + i + 1)
                    hold(dve)
                    nc.vector.bn_aggr(moments[:, i], stats[:, i]).then_inc(moments_ready, 1)
                dve.wait_ge(moments_ready, count * k + count)
                nc.vector.tensor_scalar_add(var_eps[:, 0:count], moments[:, 0:count, 1], LN_EPS).then_inc(var_ready, 1)

            def layer_norm(k, dst, src, i, rstd_ready, normed):
                dve.wait_ge(rstd_ready, k + 1)
                nc.vector.tensor_scalar(dst, src, moments[:, i, 0:1], rstd[:, i:i + 1], ALU.subtract, ALU.mult).then_inc(normed, 1)

            def stats_x(b):
                layer_stats(b, x_loaded, DMA * (b + 1), [x_in[:, i] for i in range(TT)], ln_stats, ln_moments, ln_var)

            def norm_x(b):
                for i in range(TT):
                    layer_norm(b, x_in[:, i], x_in[:, i], i, ln_rstd, ln_done)

            def split_xT(b):
                for kc in range(KC):
                    dve.wait_ge(xT_hi_ready, KC * b + kc + 1)
                    nc.vector.tensor_tensor(xT_lo[:, kc], bank[4 + kc][:], xT_hi[:, kc].bitcast(F32), ALU.subtract).then_inc(xT_ready, 1)

            def split_weights(j):
                hi, lo = w_hi[:, j], w_lo[:, j]
                dve.wait_ge(w_loaded[j % 2], DMA * (j // 2 + 1))
                if j == WBLOCKS - 1:
                    dve.wait_ge(v_norm_ready, 1)
                    nc.vector.reciprocal(inv_rms[:, 1], raw[:, QC + KVC - 1]).then_inc(v_inv_ready, 1)
                    dve.wait_ge(v_inv_ready, 1)
                    nc.vector.tensor_tensor(w_stage[:, 1], w_stage[:, 1], inv_rms[:, 1:2].broadcast_to([P, KC, T]), ALU.mult).then_inc(v_scaled, 1)
                    dve.wait_ge(v_scaled, 1)
                nc.vector.tensor_copy(hi, w_stage[:, j % 2]).then_inc(w_hi_ready, 1)
                dve.wait_ge(w_hi_ready, j + 1)
                nc.vector.tensor_tensor(lo, w_stage[:, j % 2], hi.bitcast(F32), ALU.subtract).then_inc(w_ready, 1)

            def split_raw(b, f):
                dve.wait_ge(qk_hi_ready, (QC + KVC) * b + f + 1)
                nc.vector.tensor_tensor(qk[:, f % QK_RING, 1], raw[:, f], qk[:, f % QK_RING, 0].bitcast(F32), ALU.subtract).then_inc(qk_ready, 1)

            def norm(b, f):
                dve.wait_ge(inv_ready, 2 * b + f // QC + 1)
                nc.vector.scalar_tensor_tensor(raw[:, f], raw[:, f], norm_w[:, f:f + 1], inv_rms[:, f // QC],
                                               ALU.mult, ALU.mult).then_inc(scaled, 1)
                if f:
                    split_raw(b, f - 1)
                if f == QC + KVC - 1:
                    split_raw(b, f)

            def project(b, last=False):
                first = isinstance(b, int) and b == 0
                for kind, n in SCHEDULE:
                    if kind == "norm":
                        norm(b, n)
                    elif kind == "late norm":
                        if not first:
                            norm(b - 1, n)
                    elif kind == "root":
                        dve.wait_ge(root_ready, 2 * b + n + 1)
                        nc.vector.reciprocal(inv_rms[:, n], inv_rms[:, n]).then_inc(inv_ready, 1)
                    elif n < QC + KVC:
                        if first and n == 0:
                            split_weights(0)
                        if first and n % 4 == 1:
                            split_weights(n // 4 + 1)
                        if not last and n == QC:
                            stats_x(b + 1)
                        if n not in (0, QC):
                            m = n - 1 - n // QC
                            dve.wait_ge(sq_ready, (QC + KVC) * b + n + 1)
                            at_least(dve, acc_ready, NSQ * b + m)
                            nc.vector.tensor_tensor(sum_sq[:, n // QC], sum_sq[:, n // QC], square[:, m % 2], ALU.add).then_inc(acc_ready, 1)
                        if not last and n == QC + KVC - 1:
                            norm_x(b + 1)
                    else:
                        if n == NGEMM - 1 and not last:
                            split_xT(b + 1)
                        dve.wait_ge(v_hi_ready, TT * b + n - QC - KVC + 1)
                        nc.vector.tensor_tensor(v_out[:, (n - QC) % 2, :, 1], bank[n % 4][:].rearrange("p (g d) -> p g d", g=G), v_out[:, (n - QC) % 2, :, 0],
                                                ALU.subtract).then_inc(v_ready, 1)

            stats_x(0)
            norm_x(0)
            dve.wait_ge(norm_loaded, 2 * DMA)
            nc.vector.tensor_scalar_mul(norm_w[:, 0:QC], qn_raw[:], -HD ** -0.5).then_inc(norm_ready, 1)
            split_xT(0)
            dve.wait_ge(norm_ready, 1)
            project(0)
            with dve.Fori(1, B - 1) as b:
                project(b)
            project(B - 1, last=True)

            def add_bias(n, u):
                A, i = UNITS * n + u, u // REP % TT
                _, tiles, at = window(i)
                w = P * tiles
                if u % (UNITS // 2) == 0:
                    dve.wait_ge(bias_ready, 2 * n + 2 * u // UNITS + 1)
                dve.wait_ge(s_psum, A + 1)
                at_least(dve, p_ready, A - RING + 1)
                hold(dve)
                nc.vector.tensor_tensor_reduce(out=u_sb[:, u % RING, 0:w], in0=bank[u % 2][:, 0:w],
                                               in1=bias[:, 2 * u // UNITS, u % REP, at:at + w], scale=1.0, scalar=BIG,
                                               op0=ALU.add, op1=ALU.min, accum_out=low[:, u % RING:u % RING + 1]).then_inc(u_ready, 1)

            def split_pT(n, u):
                w = P * window(u // REP % TT)[1]
                dve.wait_ge(pT_hi_ready, UNITS * n + u + 1)
                nc.vector.tensor_tensor(pT_lo[:, u % RING, 0:w], bank[2 + u % 2][:, 0:w], pT_hi[:, u % RING, 0:w],
                                        ALU.subtract).then_inc(pT_ready, 1)

            def invert_sums(n, u):
                a = 2 * TT * n + u // REP
                dve.wait_ge(p_ready, UNITS * n + u + 1)
                at_least(dve, o_mid_ready, a - 1)
                nc.vector.reciprocal(inv_sum[:, u // REP % 2], p_sum[:, u // REP % TT]).then_inc(inv_sum_ready, 1)

            def add_low(n, u):
                a = 2 * TT * n + u // REP
                dve.wait_ge(o_low_ready, a + 1)
                at_least(dve, o_mid_ready, a - 1)
                nc.vector.tensor_tensor(o_raw[:, u // REP % 2],
                                        bank[4 + u // REP % 2][:].rearrange("p (r t d) -> p r t d", r=REP, t=2)[:, :, 0],
                                        o_low[:], ALU.add).then_inc(o_raw_ready, 1)

            def split_oT(t, m):
                dve.wait_ge(oT_hi_ready, 4 * t + m + 1)
                nc.vector.tensor_tensor(oT_lo[:, m % 2].rearrange("p c n -> p (c n)"), bank[6][:],
                                        oT_hi[:, m % 2].rearrange("p c n -> p (c n)").bitcast(F32), ALU.subtract).then_inc(oT_ready, 1)

            def stats_y(t, acc):
                layer_stats(t, oT_used, 4 * t + 4, [acc[:]], y_stats, y_moments, y_var)

            def norm_y(t, acc):
                at_least(dve, z_ready, t)
                layer_norm(t, y_n[:], acc[:], 0, y_rstd, y_normed)

            def attend(n, tile=None):
                for u in range(UNITS):
                    add_bias(n, u)
                    for lag, work in ((2, split_pT), (1, invert_sums), (6, add_low)):
                        nn, uu = (n, u - lag) if u >= lag else (n - 1, UNITS + u - lag)
                        if not (isinstance(nn, int) and nn < 0) and (work is split_pT or uu % REP == REP - 1):
                            work(nn, uu)
                    if isinstance(n, int) and n == 0 and u + LATE < QC + KVC:
                        norm(B - 1, u + LATE)
                    m, at = divmod(u - START - 2, STEP)
                    if tile is not None and m in range(4) and at == 0:
                        split_oT(tile, m)
                    if u == START and tile is not None and not (isinstance(tile, int) and tile == 0):
                        norm_y(tile - 1, bank[7])
                if tile is not None:
                    stats_y(tile, bank[7])

            attention_loops(dve, attend)
            invert_sums(B * TT - 1, UNITS - 1)
            split_pT(B * TT - 1, UNITS - 2)
            add_low(B * TT - 1, UNITS - 1 - REP)
            split_pT(B * TT - 1, UNITS - 1)
            add_low(B * TT - 1, UNITS - 1)

            def finish_tile(t, acc, acc_before):
                for m in range(4):
                    split_oT(t, m)
                    if m == 0:
                        norm_y(t - 1, acc_before)
                stats_y(t, acc)

            finish_tile(B * TT - LAG, bank[5], bank[7])
            with dve.Fori(0, TT // 2) as i:
                finish_tile(B * TT - TT + 2 * i, bank[7], bank[5])
                finish_tile(B * TT - TT + 1 + 2 * i, bank[5], bank[7])
            norm_y(B * TT - 1, bank[5])

            def stats_z(m):
                layer_stats(m, z_loaded, DMA * (m + 1), [z_in[:, i] for i in range(TT)], z_stats, z_moments, z_var)

            def norm_z(m):
                for i in range(TT):
                    layer_norm(m, z_in[:, i], z_in[:, i], i, z_rstd, z_normed)

            def split_zT(m):
                for kc in range(KC):
                    dve.wait_ge(zT_hi_ready, KC * m + kc + 1)
                    nc.vector.tensor_tensor(zT_lo[:, kc], bank[kc][:], zT_hi[:, kc].bitcast(F32), ALU.subtract).then_inc(zT_ready, 1)

            def feed_forward(m, last=False):
                first = isinstance(m, int) and m == 0
                for c in range(IC):
                    C = IC * m + c
                    if first and c % PIECE == 0:
                        for j in range(c, c + 3):
                            src, hi, lo = piece(j)
                            dve.wait_ge(f_hi_ready, j + 1)
                            nc.vector.tensor_tensor(lo, src, hi.bitcast(F32), ALU.subtract).then_inc(f_ready, 1)
                    if not last and c == IC - 2:
                        stats_z(m + 1)
                    if not last and c == IC - 1:
                        norm_z(m + 1)
                    dve.wait_ge(gu_psum, 2 * C + 2)
                    dve.wait_ge(silu_ready, C + 1)
                    at_least(dve, h_ready, C)
                    nc.vector.scalar_tensor_tensor(hid[:], bank[2 * (c % 2) + 1][:], up_sc[:, c:c + 1], silu[:],
                                                   ALU.mult, ALU.mult).then_inc(hid_ready, 1)
                    dve.wait_ge(h_hi_ready, C + 1)
                    nc.vector.tensor_tensor(h_lo[:, c % 2], hid[:], h_hi[:, c % 2].bitcast(F32), ALU.subtract).then_inc(h_ready, 1)
                if not last:
                    split_zT(m + 1)
                dve.wait_ge(down_done, IC * (m + 1))
                at_least(dve, out_stored, DMA * m)
                for i in range(TT):
                    nc.vector.tensor_tensor(y_s[:, i], bank[4 + i][:], down_sc[:], ALU.mult).then_inc(ys_ready, 1)
                layer_stats(m, ys_ready, TT * (m + 1), [y_s[:, i] for i in range(TT)], f_stats, f_moments, f_var)
                for i in range(TT):
                    layer_norm(m, y_s[:, i], y_s[:, i], i, f_rstd, f_normed)

            stats_z(0)
            norm_z(0)
            split_zT(0)
            dve.wait_ge(scales_loaded, 3 * DMA)
            feed_forward(0)
            with dve.Fori(1, B - 1) as m:
                feed_forward(m)
            feed_forward(B - 1, last=True)

        @block.tensor
        def _(pe):
            pe.wait_ge(const_ready, CONSTANTS)

            def transpose_x(b):
                pe.wait_ge(ln_done, TT * b + TT)
                at_least(pe, root_ready, 2 * b)
                for kc in range(KC):
                    for i in range(TT):
                        last = nc.tensor.transpose(bank[4 + kc][:, P * i:P * i + P], x_in[:, i, P * kc:P * kc + P], ident[:])
                    last.then_inc(xT_psum, 1)

            def sum_squares(b, n):
                pe.wait_ge(acc_ready, NSQ * b + (NSQ if n else QC - 1))
                pe.wait_ge(sq_ready, (QC + KVC) * b + (QC + KVC if n else QC))
                at_least(pe, root_ready, 2 * (b - 1) + n + 1)
                if n and isinstance(b, int) and b == 0:
                    pe.wait_ge(v_norm_ready, 1)
                nc.tensor.matmul(bank[6 + n][:], ones[:], sum_sq[:, n], start=True, stop=True).then_inc(ssq_psum, 1)

            def project(b, last=False):
                first = isinstance(b, int) and b == 0
                for n in range(NGEMM):
                    if first and n == QC:
                        for kc in range(KC):
                            pe.wait_ge(v_squared, kc + 1)
                            mm = nc.tensor.matmul(bank[7][:], ones[:], raw[:, QC + kc], start=(kc == 0), stop=(kc == KC - 1))
                        mm.then_inc(v_norm_psum, 1)
                    if first and n % 4 == 0:
                        pe.wait_ge(w_ready, n // 4 + 1)
                    if n < 4:
                        at_least(pe, v_ready, TT * (b - 1) + n + 1)
                    else:
                        pe.wait_ge(sq_ready, (QC + KVC) * b + n - 4 + 1)
                    if n == NGEMM - 1 and not last:
                        transpose_x(b + 1)
                    for kc in range(KC):
                        if n == 0:
                            pe.wait_ge(xT_ready, KC * b + kc + 1)
                        if n < QC + KVC:
                            j, cols = n // TT, slice(P * (n % TT), P * (n % TT) + P)
                            parts = part_products(w_hi[:, j, kc, cols], w_lo[:, j, kc, cols], xT_hi[:, kc], xT_lo[:, kc])
                        else:
                            i = n - QC - KVC
                            tokens = slice(P * i, P * i + P)
                            parts = part_products(xT_hi[:, kc, tokens], xT_lo[:, kc, tokens], w_hi[:, WBLOCKS - 1, kc], w_lo[:, WBLOCKS - 1, kc])
                        for k, (lhs, rhs) in enumerate(parts):
                            mm = nc.tensor.matmul(bank[n % 4][:], lhs, rhs, start=(kc == 0 and k == 0), stop=(kc == KC - 1 and k == 2))
                    mm.then_inc(gemm_done, 1)
                    if n == QC:
                        sum_squares(b, 0)
                    if n == QC + KVC:
                        sum_squares(b, 1)

            transpose_x(0)
            project(0)
            with pe.Fori(1, B - 1) as b:
                project(b)
            project(B - 1, last=True)

            def scores(n, u):
                A, s, i, r = UNITS * n + u, 2 * u // UNITS, u // REP % TT, u % REP
                key, tiles, _ = window(i)
                w = P * tiles
                if u % (UNITS // 2) == 0:
                    pe.wait_ge(heads_loaded[s], 4 * DMA * (n + 1))
                at_least(pe, u_ready, A - 1)
                for part in range(2):
                    mm = nc.tensor.matmul(bank[u % 2][:, 0:w], q_st[:, s, r, P * i:P * i + P],
                                          k_st[:, s, part, P * key:P * key + w], start=(part == 0), stop=(part == 1))
                mm.then_inc(s_psum, 1)

            def transpose_p(n, u):
                A, tiles = UNITS * n + u, window(u // REP % TT)[1]
                pe.wait_ge(p_ready, A + 1)
                at_least(pe, pT_ready, A - 1)
                for j in range(tiles):
                    mm = nc.tensor.transpose(bank[2 + u % 2][:, P * j:P * j + P], p_sb[:, u % RING, P * j:P * j + P], ident[:])
                mm.then_inc(pT_psum, 1)

            def weigh_values(n, u):
                A, s, r, ring = UNITS * n + u, 2 * u // UNITS, u % REP, u % RING
                key, tiles, _ = window(u // REP % TT)
                acc = bank[4 + u // REP % 2][:, 2 * HD * r:2 * HD * r + 2 * HD]
                pe.wait_ge(pT_ready, A + 1)
                if r == 0:
                    at_least(pe, o_raw_ready, 2 * TT * n + u // REP - 1)
                for j in range(tiles):
                    nc.tensor.matmul(acc, pT_hi[:, ring, P * j:P * j + P], v_st[:, s, key + j],
                                     start=(j == 0), stop=False, skip_group_check=True)
                    mm = nc.tensor.matmul(acc[:, 0:HD], pT_lo[:, ring, P * j:P * j + P], v_st[:, s, key + j, 0:HD],
                                          start=False, stop=(j == tiles - 1), skip_group_check=True)
                mm.then_inc(pv_done, 1)

            def transpose_o(t, m):
                if m == 0:
                    pe.wait_ge(tile_loaded, DMA * (t + 1))
                at_least(pe, oT_ready, 4 * t + m)
                for c in range(4):
                    mm = nc.tensor.transpose(bank[6][:, P * c:P * c + P], o_in[:, m, P * c:P * c + P], ident[:])
                mm.then_inc(oT_psum, 1)

            def project_o(t, m, products, acc):
                for j in products:
                    if j == 0:
                        pe.wait_ge(oT_ready, 4 * t + m + 1)
                    c, k = divmod(j, 3)
                    chunk = 4 * m + c
                    lhs, rhs = part_products(oT_hi[:, m % 2, c], oT_lo[:, m % 2, c], wo_hi[:, chunk], wo_lo[:, chunk])[k]
                    mm = nc.tensor.matmul(acc[:], lhs, rhs, start=(chunk == 0 and k == 0), stop=(chunk == QC - 1 and k == 2))
                    if j == 11:
                        mm.then_inc(oT_used, 1)

            def attend(n, tile=None):
                for u in range(UNITS):
                    scores(n, u)
                    for lag, work in ((2, transpose_p), (4, weigh_values)):
                        nn, uu = (n, u - lag) if u >= lag else (n - 1, UNITS + u - lag)
                        if not (isinstance(nn, int) and nn < 0):
                            work(nn, uu)
                    if tile is not None:
                        m, at = divmod(u - START, STEP)
                        if m in range(4) and at == 0:
                            transpose_o(tile, m)
                        m, at = divmod(u - START - 4, STEP)
                        if m in range(4):
                            if m == 0 and at == 0:
                                at_least(pe, y_normed, tile)
                                if isinstance(tile, int):
                                    pe.wait_ge(wo_ready, QC)
                            project_o(tile, m, (2 * at, 2 * at + 1), bank[7])

            pe.wait_ge(v_ready, TT * B)
            attention_loops(pe, attend)
            for u in range(UNITS - 2, UNITS):
                transpose_p(B * TT - 1, u)
            for u in range(UNITS - 4, UNITS):
                weigh_values(B * TT - 1, u)

            def finish_tile(t, acc):
                transpose_o(t, 0)
                pe.wait_ge(y_normed, t - 1)
                for m in range(4):
                    if m < 3:
                        transpose_o(t, m + 1)
                    project_o(t, m, range(12), acc)

            pe.wait_ge(o_raw_ready, 2 * TT * B * TT)
            finish_tile(B * TT - LAG, bank[5])
            with pe.Fori(0, TT // 2) as i:
                finish_tile(B * TT - TT + 2 * i, bank[7])
                finish_tile(B * TT - TT + 1 + 2 * i, bank[5])

            def transpose_z(m):
                pe.wait_ge(z_normed, TT * m + TT)
                for kc in range(KC):
                    at_least(pe, hid_ready, IC * m if kc < 2 else IC * m - 1)
                    for i in range(TT):
                        mm = nc.tensor.transpose(bank[kc][:, P * i:P * i + P], z_in[:, i, P * kc:P * kc + P], ident[:])
                    mm.then_inc(zT_psum, 1)

            def gate_and_up(m, c):
                C = IC * m + c
                for g in range(2):
                    if c:
                        at_least(pe, hid_ready, C - 1)
                    for kc in range(KC):
                        if c == 0 and g == 0:
                            pe.wait_ge(zT_ready, KC * m + KC)
                        w = [x[:, kc, g, P * c:P * c + P] for x in (gu_hi, gu_lo)]
                        for k, (lhs, rhs) in enumerate(part_products(*w, zT_hi[:, kc], zT_lo[:, kc])):
                            mm = nc.tensor.matmul(bank[2 * (c % 2) + g][:], lhs, rhs, start=(kc == 0 and k == 0), stop=(kc == KC - 1 and k == 2))
                    mm.then_inc(gu_psum, 1)

            def down(m, c):
                pe.wait_ge(h_ready, IC * m + c + 1)
                for i in range(TT):
                    if c == 0:
                        at_least(pe, ys_ready, TT * (m - 1) + i + 1)
                    h = [x[:, c % 2, P * i:P * i + P] for x in (h_hi, h_lo)]
                    for k, (lhs, rhs) in enumerate(part_products(*h, dn_hi[:, c], dn_lo[:, c])):
                        mm = nc.tensor.matmul(bank[4 + i][:], lhs, rhs, start=(c == 0 and k == 0), stop=(c == IC - 1 and k == 2))
                mm.then_inc(down_done, 1)

            def feed_forward(m, last=False):
                for c in range(IC):
                    if isinstance(m, int) and m == 0 and c % PIECE == 0:
                        pe.wait_ge(f_ready, c + 3)
                    gate_and_up(m, c)
                    if c:
                        down(m, c - 1)
                if not last:
                    transpose_z(m + 1)
                down(m, IC - 1)

            transpose_z(0)
            feed_forward(0)
            with pe.Fori(1, B - 1) as m:
                feed_forward(m)
            feed_forward(B - 1, last=True)


def kernel(L0_attn_x, L0_attn_wq, L0_attn_wk, L0_attn_wv, L0_attn_wo, L0_attn_q_norm_w, L0_attn_k_norm_w,
           L0_ffn_gate_w, L0_ffn_up_w, L0_ffn_down_w, L0_ffn_gate_s, L0_ffn_up_s, L0_ffn_down_s):
    import concourse.bacc as bacc
    from concourse.bass_utils import run_bass_kernel_spmd

    def columns(a):
        return a.reshape(-1, P).T

    arrays = {
        "x": L0_attn_x, "wqT": np.transpose(L0_attn_wq), "wkT": np.transpose(L0_attn_wk),
        "wvT": np.transpose(L0_attn_wv), "woT": np.transpose(L0_attn_wo), "q_norm": columns(L0_attn_q_norm_w),
        "k_norm": columns(L0_attn_k_norm_w), "gateT": np.transpose(L0_ffn_gate_w), "upT": np.transpose(L0_ffn_up_w),
        "downT": np.transpose(L0_ffn_down_w), "gate_s": columns(L0_ffn_gate_s), "up_s": columns(L0_ffn_up_s), "down_s": L0_ffn_down_s,
    }
    arrays = {name: np.ascontiguousarray(a) for name, a in arrays.items()}
    nc = bacc.Bacc("TRN2", target_bir_lowering=False, num_devices=1)
    args = {name: nc.dram_tensor(name, a.shape, mybir.dt.from_np(a.dtype), kind="ExternalInput").ap() for name, a in arrays.items()}
    out = nc.dram_tensor("out", (B, T, D), F32, kind="ExternalOutput").ap()
    sandwich_layer(nc, **args, out=out)
    result = run_bass_kernel_spmd(nc, [arrays], core_ids=[0])
    return result.results[0]["out"]
```

```python
from contextlib import ExitStack

import concourse.bass as bass
import numpy as np
from concourse import mybir

F32 = mybir.dt.float32
F32R = mybir.dt.float32r
F16 = mybir.dt.float16
ACT = mybir.ActivationFunctionType
ALU = mybir.AluOpType

P = 128
B, T, D = 4, 512, 512
H, G, HD = 32, 8, 64
REP = H // G
WINDOW = 256
INTER = 1408
KC = D // P
TT = T // P
QC, KVC = H * HD // P, G * HD // P
WQKV = (H + 2 * G) * HD
NB = WINDOW // P + 1
WIN = NB * P
IC = INTER // P
RMS_EPS, LN_EPS = 1e-6, 1e-5
BIG = 1e30
VSCALE = 1024.0
NGEMM = QC + KVC + TT
NSQ = QC + KVC - 2
TAIL_BANKS = (6, 4)
QK_RING = 4
LATE = 6
WBLOCKS = WQKV // T
WEIGHTS_DUE = (1, 5, 9, 13, QC + 2)
UNITS = 2 * TT * REP
LAG = TT + 1
STEP = 6
START = 2
LAGS = {"split": 3, "scores": 0, "transpose": 2, "exps": 0, "invert_sums": 1, "weigh": 4, "copy_low": 5, "add_low": 6}
OF_FOUR_HEADS = ("invert_sums", "copy_low", "add_low")
DRAIN = max(LAGS.values())
RING = 4
PIECE = 3
DMA = 16
RATIO = 2.0 ** (-8.0 / H)
TINY = 1e-30
CONSTANTS = 6


def projection_schedule():
    order, norms, late = [], iter(range(LATE)), iter(range(LATE, QC + KVC))
    for n in range(NGEMM):
        order.append(("gemm", n))
        order += [("late norm", f) for _, f in zip(range(1), late)]
        if n == QC + 2:
            order.append(("root", 0))
        if n > QC + 1:
            order += [("norm", f) for _, f in zip(range(1), norms)]
        if n == QC + KVC + 1:
            order.append(("root", 1))
    return order


def feed_forward_pieces():
    return [(kind, c, min(PIECE, IC - c)) for c in range(0, IC, PIECE) for kind in ("gate", "up", "down")]


SCHEDULE = projection_schedule()
PIECES = feed_forward_pieces()


def attention_loops(eng, attend):
    attend(0)
    with eng.Fori(1, LAG) as n:
        attend(n)
    attend(LAG, 0)
    with eng.Fori(1, TT) as i:
        attend(LAG + i, i)
    with eng.Fori(0, TT) as i:
        attend(LAG + TT + i, TT + i)
    with eng.Fori(0, TT - 1) as i:
        attend(LAG + 2 * TT + i, 2 * TT + i)


def due(n, u):
    for stage, lag in LAGS.items():
        nn, uu = (n, u - lag) if u >= lag else (n - 1, UNITS + u - lag)
        if uu < UNITS and not (isinstance(nn, int) and nn < 0) and (stage not in OF_FOUR_HEADS or uu % REP == REP - 1):
            yield stage, nn, uu


def at_least(eng, sem, value):
    if isinstance(value, int) and value <= 0:
        return
    eng.wait_ge(sem, value)


def part_products(a_hi, a_lo, b_hi, b_lo):
    return ((a_hi, b_hi), (a_lo, b_hi), (a_hi, b_lo))


def window(i):
    first = max(0, i - NB + 1)
    return first, i - first + 1, (first - i + NB - 1) * P


def qk_stores(b, f):
    return DMA * ((QC + KVC) // QK_RING * b + f // QK_RING)


def sandwich_layer(nc, x, wqT, wkT, wvT, woT, q_norm, k_norm, gateT, upT, downT, gate_s, up_s, down_s, out):
    x_t = x.rearrange("b (i p) d -> b p i d", p=P)
    out_t = out.rearrange("b (i p) d -> b p i d", p=P)
    x_flat = x.rearrange("b (i p) d -> (b i) p d", p=P)

    q_scr = nc.dram_tensor("q_scr", [B * H, HD, 2, T], F32, kind="Internal").ap()
    k_scr = nc.dram_tensor("k_scr", [B * G, HD, 2, T], F32, kind="Internal").ap()
    v_scr = nc.dram_tensor("v_scr", [B * G, P, TT, 2 * HD], F16, kind="Internal").ap()
    o_scr = nc.dram_tensor("o_scr", [B * TT, TT, P, 2 * REP * HD], F32, kind="Internal").ap()
    vn_scr = nc.dram_tensor("vn_scr", [P, G * HD], F32, kind="Internal").ap()
    z_scr = nc.dram_tensor("z_scr", [B * TT, P, D], F32, kind="Internal").ap()

    with ExitStack() as ctx:
        def sb(scope, name, shape, dt=F32):
            return scope.enter_context(nc.sbuf_tensor(name, shape, dt))

        def sem(name):
            return ctx.enter_context(nc.semaphore(name))

        def sems(names):
            return [sem(name) for name in names.split()]

        bank = [ctx.enter_context(nc.psum_tensor(f"bank{i}", [P, 512], F32)) for i in range(8)]

        ident = sb(ctx, "ident", [P, P])
        ones = sb(ctx, "ones", [P, P])
        stats = sb(ctx, "stats", [P, TT, 6])
        moments = sb(ctx, "moments", [P, TT, 2])
        var_eps = sb(ctx, "var_eps", [P, TT])
        rstd = sb(ctx, "rstd", [P, TT])
        minus_half = sb(ctx, "minus_half", [P, TT])
        eps_rms = sb(ctx, "eps_rms", [P, 1])
        eps_tiny = sb(ctx, "eps_tiny", [P, 1])
        warm = sb(ctx, "warm", [P, 1])

        dist = sb(ctx, "dist", [P, WIN])
        slopes = sb(ctx, "slopes", [P, H + 4 * REP])

        with ExitStack() as s1:
            w_hi = sb(s1, "w_hi", [P, WBLOCKS, KC, T], F32R)
            w_lo = sb(s1, "w_lo", [P, WBLOCKS, KC, T], F32R)
            xT_hi = sb(s1, "xT_hi", [P, KC, T], F32R)
            xT_lo = sb(s1, "xT_lo", [P, KC, T], F32R)
            x_in = sb(s1, "x_in", [P, TT, D])
            raw = sb(s1, "raw", [P, QC + KVC, T])
            square = sb(s1, "square", [P, 2, T])
            sum_sq = sb(s1, "sum_sq", [P, 2, T])
            inv_rms = sb(s1, "inv_rms", [P, 2, T])
            v_out = sb(s1, "v_out", [P, G, TT, 2, HD], F16)
            qn_raw = sb(s1, "qn_raw", [P, QC])
            norm_w = sb(s1, "norm_w", [P, QC + KVC])
            with ExitStack() as before_norms:
                w_stage = sb(before_norms, "w_stage", [P, 2, KC, T])
            qk = sb(s1, "qk", [P, QK_RING, 2, T], F32R)

        with ExitStack() as s2:
            q_st = sb(s2, "q_st", [P, 2, REP, T], F32R)
            k_st = sb(s2, "k_st", [P, 2, 2, T], F32R)
            v_st = sb(s2, "v_st", [P, 2, TT, 2 * HD], F16)
            bias = sb(s2, "bias", [P, 2, REP, WIN])
            v_norm = sb(s2, "v_norm", [P, G + 2, HD])
            u_sb = sb(s2, "u_sb", [P, RING, WIN])
            low = sb(s2, "low", [P, RING])
            p_sb = sb(s2, "p_sb", [P, RING, WIN])
            pT_hi = sb(s2, "pT_hi", [P, RING, WIN], F16)
            pT_lo = sb(s2, "pT_lo", [P, RING, WIN], F16)
            p_sum = sb(s2, "p_sum", [P, TT, REP])
            inv_sum = sb(s2, "inv_sum", [P, 2, REP])
            o_low = sb(s2, "o_low", [P, REP, HD])
            o_raw = sb(s2, "o_raw", [P, 2, REP, HD])
            o_mid = sb(s2, "o_mid", [P, REP, HD])
            o_out = sb(s2, "o_out", [P, TT, REP, HD])
            wo_stage = sb(s2, "wo_stage", [P, TT, D])
            wo_hi = sb(s2, "wo_hi", [P, QC, D], F32R)
            wo_lo = sb(s2, "wo_lo", [P, QC, D], F32R)
            o_in = sb(s2, "o_in", [P, TT, 2 * REP * HD])
            oT_hi = sb(s2, "oT_hi", [P, 2, 4, P], F32R)
            oT_lo = sb(s2, "oT_lo", [P, 2, 4, P], F32R)
            x_res = sb(s2, "x_res", [P, D])
            y_n = sb(s2, "y_n", [P, D])
            z_out = sb(s2, "z_out", [P, D])

        with ExitStack() as s4:
            f_stage = sb(s4, "f_stage", [P, 2, KC * PIECE * P])
            gu = [sb(s4, "gu0", [P, 2, KC, 2, PIECE * P], F32R)]
            dn = [sb(s4, "dn0", [P, 2, PIECE, D], F32R)]
            gate_sc = sb(s4, "gate_sc", [P, IC])
            up_sc = sb(s4, "up_sc", [P, IC])
            down_sc = sb(s4, "down_sc", [P, D])
            zT_hi = sb(s4, "zT_hi", [P, KC, T], F32R)
            zT_lo = sb(s4, "zT_lo", [P, KC, T], F32R)
            z_in = sb(s4, "z_in", [P, TT, D])
            lo_counts = sb(s4, "lo_counts", [P, len(PIECES)])
            lo_count = sb(s4, "lo_count", [P, 1])
            lo_total = sb(s4, "lo_total", [1, 1])
            silu = sb(s4, "silu", [P, T])
            hid = sb(s4, "hid", [P, T])
            h_hi = sb(s4, "h_hi", [P, 2, T], F32R)
            h_lo = sb(s4, "h_lo", [P, 2, T], F32R)
            for at in range(PIECE, IC, PIECE):
                size = min(PIECE, IC - at)
                gu.append(sb(s4, f"gu{at // PIECE}", [P, 2, KC, 2, size * P], F32R))
                dn.append(sb(s4, f"dn{at // PIECE}", [P, 2, size, D], F32R))
            y_s = sb(s4, "y_s", [P, TT, D])
            z_res = sb(s4, "z_res", [P, TT, D])

        const_ready, x_loaded, norm_loaded, norm_ready, vn_stored = sems(
            "const_ready x_loaded norm_loaded norm_ready vn_stored")
        w_loaded = sems("w_loaded0 w_loaded1")
        w_hi_ready, w_ready, v_squared, v_norm_psum, v_norm_ready, v_inv_ready, v_scaled = sems(
            "w_hi_ready w_ready v_squared v_norm_psum v_norm_ready v_inv_ready v_scaled")
        ln_stats, ln_moments, ln_var, ln_rstd, ln_done = sems("ln_stats ln_moments ln_var ln_rstd ln_done")
        xT_psum, xT_hi_ready, xT_ready, gemm_done = sems("xT_psum xT_hi_ready xT_ready gemm_done")
        raw_ready, sq_ready, acc_ready, ssq_psum, root_ready, inv_ready = sems(
            "raw_ready sq_ready acc_ready ssq_psum root_ready inv_ready")
        scaled, qk_hi_ready, qk_ready, v_hi_ready, v_ready = sems("scaled qk_hi_ready qk_ready v_hi_ready v_ready")
        qk_stored, v_stored = sems("qk_stored0 qk_stored1 qk_stored2 qk_stored3"), sem("v_stored")
        held = sem("held")
        heads_loaded, o_stored, wo_loaded = sems("heads_loaded0 heads_loaded1"), sems("o_stored0 o_stored1 o_stored2 o_stored3"), sem("wo_loaded")
        dist_ready, bias_ready, vn_loaded = sems("dist_ready bias_ready vn_loaded")
        s_psum, u_ready, p_ready, pT_psum, pT_hi_ready, pT_ready, pv_done = sems(
            "s_psum u_ready p_ready pT_psum pT_hi_ready pT_ready pv_done")
        inv_sum_ready, o_low_ready, o_raw_ready, o_mid_ready, o_ready = sems(
            "inv_sum_ready o_low_ready o_raw_ready o_mid_ready o_ready")
        wo_hi_ready, wo_ready, tile_loaded, res1_loaded, oT_psum, oT_hi_ready, oT_ready, oT_used = sems(
            "wo_hi_ready wo_ready tile_loaded res1_loaded oT_psum oT_hi_ready oT_ready oT_used")
        y_stats, y_moments, y_var, y_rstd, y_normed, z_ready, z_stored = sems(
            "y_stats y_moments y_var y_rstd y_normed z_ready z_stored")
        lo_ready, lo_counted, lo_summed = sems("lo_ready lo_counted lo_summed")
        f_loaded = sems("f_loaded0 f_loaded1")
        f_hi_ready, f_ready, scales_loaded, z_loaded, z_stats, z_moments, z_var, z_rstd, z_normed = sems(
            "f_hi_ready f_ready scales_loaded z_loaded z_stats z_moments z_var z_rstd z_normed")
        zT_psum, zT_hi_ready, zT_ready, gu_psum, silu_ready, hid_ready, h_hi_ready, h_ready = sems(
            "zT_psum zT_hi_ready zT_ready gu_psum silu_ready hid_ready h_hi_ready h_ready")
        down_done, ys_ready, f_stats, f_moments, f_var, f_rstd, f_normed, f_sum, res_loaded, out_stored = sems(
            "down_done ys_ready f_stats f_moments f_var f_rstd f_normed f_sum res_loaded out_stored")

        def piece(j):
            kind, at, size = PIECES[j]
            if kind == "down":
                src = f_stage[:, j % 2, 0:size * D].rearrange("p (c d) -> p c d", c=size)
                return (src, *(dn[at // PIECE][:, part] for part in range(2)))
            src = f_stage[:, j % 2, 0:KC * P * size].rearrange("p (k n) -> p k n", k=KC)
            g = ("gate", "up").index(kind)
            return (src, *(gu[at // PIECE][:, part, :, g] for part in range(2)))

        block = ctx.enter_context(nc.Block())

        def hold(eng):
            eng.sem_inc(held, 1)

        @block.sync
        def _(sp):
            w_src = [wqT[:, T * j:T * j + T] for j in range(H * HD // T)] + [wkT, wvT]

            def load_weights(j):
                at_least(sp, w_ready, j - 1)
                sp.dma_start(w_stage[:, j % 2], w_src[j].rearrange("(k p) n -> p k n", p=P)).then_inc(w_loaded[j % 2], DMA)

            sp.dma_start(x_in[:], x_t[0]).then_inc(x_loaded, DMA)
            load_weights(0)
            sp.dma_start(qn_raw[:], q_norm).then_inc(norm_loaded, DMA)
            sp.dma_start(norm_w[:, QC:], k_norm).then_inc(norm_loaded, DMA)
            for j in range(1, WBLOCKS):
                load_weights(j)

            def project(b, last=False):
                if not last:
                    sp.wait_ge(xT_psum, KC * b + KC)
                    sp.dma_start(x_in[:], x_t[bass.ds(b + 1, 1)].rearrange("a p i d -> p (a i) d")).then_inc(x_loaded, DMA)
                for kind, n in SCHEDULE:
                    if kind == "gemm" and n == QC + 1 and isinstance(b, int) and b == 0:
                        sp.wait_ge(v_norm_ready, 1)
                        sp.dma_start(vn_scr, raw[:, QC + KVC - 1]).then_inc(vn_stored, DMA)
                    if kind == "gemm" and n == NGEMM - 1:
                        sp.wait_ge(v_ready, TT * b + TT)
                        sp.dma_start(v_scr[bass.ds(b * G, G)].rearrange("g p i n -> p g (i n)"),
                                     v_out[:].rearrange("p g i t d -> p g (i t d)")).then_inc(v_stored, DMA)
                    if kind == "root" and n == 0 and last:
                        stage1_stored(b)
                        sp.wait_ge(vn_stored, DMA)
                        sp.wait_ge(gemm_done, NGEMM * b + QC)
                        load_heads(0, 0)
                        load_heads(0, 1)
                    if kind == "norm":
                        store_qk(b, n)
                    if kind == "late norm" and not (isinstance(b, int) and b == 0):
                        store_qk(b - 1, n)

            def store_qk(b, f):
                sp.wait_ge(qk_ready, (QC + KVC) * b + f + 1)
                scr, head = (q_scr, b * H + 2 * f) if f < QC else (k_scr, b * G + 2 * (f - QC))
                sp.dma_start(scr[bass.ds(head, 2)].rearrange("h d t n -> (h d) t n"),
                             qk[:, f % QK_RING].bitcast(F32)).then_inc(qk_stored[f % QK_RING], DMA)

            def stage1_stored(batches):
                for s in range(QK_RING):
                    sp.wait_ge(qk_stored[s], qk_stores(batches, 0))
                sp.wait_ge(v_stored, DMA * batches)

            def load_heads(n, s):
                at_least(sp, pv_done, UNITS * (n - 1) + UNITS // 2 * (s + 1))
                g = 2 * n + s
                for copy in range(2):
                    sp.dma_start(k_st[copy:P:2, s].bitcast(F32),
                                 k_scr[bass.ds(g, 1)].rearrange("a d t n -> (a d) t n")).then_inc(heads_loaded[s], DMA)
                sp.dma_start(q_st[:, s].bitcast(F32),
                             q_scr[bass.ds(g * REP, REP)].rearrange("h d t n -> (d t) h n")).then_inc(heads_loaded[s], DMA)
                sp.dma_start(v_st[:, s],
                             v_scr[bass.ds(g, 1)].rearrange("a p i n -> (a p) i n")).then_inc(heads_loaded[s], DMA)

            project(0)
            with sp.Fori(1, B - 1) as b:
                project(b)
            project(B - 1, last=True)

            def store_o(n, s, tiles):
                for i in tiles:
                    sp.wait_ge(o_ready, 2 * TT * n + TT * s + i + 1)
                    sp.dma_start(o_scr[bass.ds(n, 1), i, :, s * REP * HD:(s + 1) * REP * HD].rearrange("a p c -> (a p) c"),
                                 o_out[:, i].rearrange("p r d -> p (r d)")).then_inc(o_stored[i], DMA)

            def load_o(b, i):
                at_least(sp, oT_psum, 4 * (TT * b + i))
                sp.dma_start(o_in[:], o_scr[bass.ds(b * TT, TT), bass.ds(i, 1)].rearrange("g a p c -> p (g a) c")).then_inc(tile_loaded, DMA)

            def load_residual(t):
                at_least(sp, z_ready, t)
                sp.dma_start(x_res[:], x_flat[bass.ds(t, 1)].rearrange("a p d -> (a p) d")).then_inc(res1_loaded, DMA)

            def store_z(t):
                sp.wait_ge(z_ready, t + 1)
                sp.dma_start(z_scr[bass.ds(t, 1)].rearrange("a p d -> (a p) d"), z_out[:]).then_inc(z_stored, DMA)

            def load_wo(group):
                at_least(sp, wo_ready, TT * group)
                hold(sp)
                sp.dma_start(wo_stage[:], woT.rearrange("(g c p) d -> g p c d", g=QC // TT, p=P)[bass.ds(group, 1)]
                             .rearrange("a p c d -> p (a c) d")).then_inc(wo_loaded, DMA)

            def attend(n, tile=None, wo=False):
                store_o(n - 1, 0, [TT - 1])
                load_heads(n, 0)
                if tile is not None:
                    for i in range(TT):
                        sp.wait_ge(o_stored[i], DMA * (2 * n - 1))
                    hold(sp)
                    load_o(*tile)
                store_o(n - 1, 1, range(TT - 1))
                load_heads(n, 1)
                store_o(n - 1, 1, [TT - 1])
                if wo:
                    load_wo(n - 1)
                store_o(n, 0, [0])
                if tile is not None:
                    t = TT * tile[0] + tile[1]
                    if not isinstance(t, int):
                        store_z(t - 1)
                    load_residual(t)
                store_o(n, 0, range(1, TT - 1))

            sp.wait_ge(gemm_done, NGEMM * B)
            sp.dma_start(v_norm[:, 0:G].rearrange("p g d -> p (g d)"), vn_scr).then_inc(vn_loaded, DMA)
            sp.dma_start(v_norm[:, G:G + 2].rearrange("p g d -> p (g d)"), vn_scr[:, 0:2 * HD]).then_inc(vn_loaded, DMA)
            for f in range(LATE, QC + KVC):
                store_qk(B - 1, f)
            stage1_stored(B)
            store_o(0, 0, range(TT - 1))
            with sp.Fori(1, LAG) as n:
                attend(n, wo=True)
            attend(LAG, (0, 0))
            with sp.Fori(1, TT) as i:
                attend(LAG + i, (0, i))
            with sp.Fori(0, TT) as i:
                attend(LAG + TT + i, (1, i))
            with sp.Fori(0, TT - 1) as i:
                attend(LAG + 2 * TT + i, (2, i))
            for i in range(TT):
                sp.wait_ge(o_stored[i], DMA * (2 * B * TT - 1 - (i == TT - 1)))
            load_o(B - 2, TT - 1)
            store_o(B * TT - 1, 0, [TT - 1])
            store_o(B * TT - 1, 1, range(TT))
            for i in range(TT):
                sp.wait_ge(o_stored[i], DMA * 2 * B * TT)

            def load_z(tile, m, done):
                sp.dma_start(tile[:], z_scr[bass.ds(TT * m, TT)].rearrange("i p d -> p i d")).then_inc(done, DMA)

            def load_piece(j):
                kind, at, size = PIECES[j]
                at_least(sp, f_ready, j - 1)
                if kind == "down":
                    src = downT[P * at:P * (at + size), :].rearrange("(c p) d -> p c d", p=P)
                    dst = f_stage[:, j % 2, 0:size * D].rearrange("p (c d) -> p c d", c=size)
                else:
                    src = (gateT if kind == "gate" else upT)[:, P * at:P * (at + size)].rearrange("(k p) n -> p k n", p=P)
                    dst = f_stage[:, j % 2, 0:KC * P * size].rearrange("p (k n) -> p k n", k=KC)
                sp.dma_start(dst, src).then_inc(f_loaded[j % 2], DMA)

            sp.wait_ge(z_stored, DMA * (B * TT - LAG - 1))
            load_z(z_in, 0, z_loaded)
            load_piece(0)
            load_piece(1)
            sp.dma_start(gate_sc[:], gate_s).then_inc(scales_loaded, DMA)
            sp.dma_start(up_sc[:], up_s).then_inc(scales_loaded, DMA)
            sp.dma_start(down_sc[:], down_s.partition_broadcast(P)).then_inc(scales_loaded, DMA)
            with sp.Fori(0, TT) as i:
                store_z(TT * (B - 1) + i - 2)
                load_residual(TT * (B - 1) + i - 1)
                load_o(B - 1, i)
            load_piece(2)
            store_z(B * TT - 2)
            load_residual(B * TT - 1)
            store_z(B * TT - 1)
            sp.wait_ge(z_stored, DMA * B * TT)

            for j in range(3, len(PIECES)):
                load_piece(j)

            def feed_forward(m, last=False):
                if not last:
                    sp.wait_ge(zT_psum, KC * m + KC)
                    load_z(z_in, m + 1, z_loaded)
                at_least(sp, f_sum, TT * m)
                load_z(z_res, m, res_loaded)
                sp.wait_ge(f_sum, TT * m + TT)
                sp.dma_start(out_t[bass.ds(m, 1)].rearrange("a p i d -> p (a i) d"), y_s[:]).then_inc(out_stored, DMA)

            feed_forward(0)
            with sp.Fori(1, B - 1) as m:
                feed_forward(m)
            feed_forward(B - 1, last=True)
            sp.wait_ge(out_stored, DMA * B)

        @block.gpsimd
        def _(pool):
            nc.gpsimd.memset(ident[:], 0.0).then_inc(const_ready, 1)
            nc.gpsimd.memset(ones[:], 1.0).then_inc(const_ready, 1)
            nc.gpsimd.memset(minus_half[:], -0.5).then_inc(const_ready, 1)
            nc.gpsimd.memset(eps_rms[:], RMS_EPS).then_inc(const_ready, 1)
            nc.gpsimd.memset(eps_tiny[:], TINY).then_inc(const_ready, 1)
            pool.wait_ge(const_ready, 5)
            nc.gpsimd.affine_select(out=ident[:], in_=ident[:], compare_op=ALU.not_equal, fill=1.0, base=0,
                                    pattern=[[-1, P]], channel_multiplier=1).then_inc(const_ready, 1)

            def inverse_root(count, var_ready, value, done):
                pool.wait_ge(var_ready, value)
                nc.gpsimd.tensor_tensor(out=rstd[:, 0:count], in0=var_eps[:, 0:count], in1=minus_half[:, 0:count],
                                        op=ALU.pow).then_inc(done, 1)

            inverse_root(TT, ln_var, 1, ln_rstd)

            nc.gpsimd.iota(dist[:], pattern=[[-1, WIN]], base=WINDOW, channel_multiplier=1,
                           allow_small_or_imprecise_dtypes=True).then_inc(dist_ready, 1)
            for h in range(H + 4 * REP):
                nc.gpsimd.memset(slopes[:, h:h + 1], float(np.float32(RATIO ** (h % H)))).then_inc(dist_ready, 1)
            pool.wait_ge(dist_ready, 1 + H + 4 * REP)
            nc.gpsimd.affine_select(out=dist[:], in_=dist[:], compare_op=ALU.is_ge, fill=BIG, base=WINDOW,
                                    pattern=[[-1, WIN]], channel_multiplier=1).then_inc(dist_ready, 1)
            pool.wait_ge(dist_ready, 2 + H + 4 * REP)
            nc.gpsimd.affine_select(out=dist[:], in_=dist[:], compare_op=ALU.is_ge, fill=BIG, base=0,
                                    pattern=[[1, WIN]], channel_multiplier=-1).then_inc(dist_ready, 1)
            pool.wait_ge(dist_ready, 3 + H + 4 * REP)

            with pool.Fori(1, B) as b:
                inverse_root(TT, ln_var, b + 1, ln_rstd)

            def make_bias(n, q, s):
                at_least(pool, u_ready, UNITS * (n - 1) + UNITS // 2 * (s + 1))
                hold(pool)
                nc.gpsimd.tensor_tensor(out=bias[:, s], in0=dist[:].unsqueeze(1).broadcast_to([P, REP, WIN]),
                                        in1=slopes[:, bass.ds(2 * REP * q + REP * s, REP)].unsqueeze(2).broadcast_to([P, REP, WIN]),
                                        op=ALU.mult).then_inc(bias_ready, 1)

            def finish_o(n, q, s, i):
                a = 2 * TT * n + TT * s + i
                pool.wait_ge(inv_sum_ready, a + 1)
                pool.wait_ge(o_raw_ready, a + 1)
                at_least(pool, o_ready, a)
                nc.gpsimd.tensor_tensor(out=o_mid[:], in0=o_raw[:, i % 2],
                                        in1=inv_sum[:, i % 2].unsqueeze(2).broadcast_to([P, REP, HD]),
                                        op=ALU.mult).then_inc(o_mid_ready, 1)
                pool.wait_ge(o_mid_ready, a + 1)
                at_least(pool, o_stored[i], DMA * (2 * n + s))
                hold(pool)
                nc.gpsimd.tensor_tensor(out=o_out[:, i], in0=o_mid[:],
                                        in1=v_norm[:, bass.ds(2 * q + s, 1)].broadcast_to([P, REP, HD]),
                                        op=ALU.mult).then_inc(o_ready, 1)

            def split_wo(group, i):
                chunk = bass.ds(TT * group + i, 1)
                pool.wait_ge(wo_loaded, DMA * (group + 1))
                hold(pool)
                nc.gpsimd.tensor_copy(wo_hi[:, chunk], wo_stage[:, i:i + 1]).then_inc(wo_hi_ready, 1)
                pool.wait_ge(wo_hi_ready, TT * group + i + 1)
                hold(pool)
                nc.gpsimd.tensor_tensor(out=wo_lo[:, chunk], in0=wo_stage[:, i:i + 1], in1=wo_hi[:, chunk].bitcast(F32),
                                        op=ALU.subtract).then_inc(wo_ready, 1)

            def add_residual(t):
                pool.wait_ge(y_normed, t + 1)
                pool.wait_ge(res1_loaded, DMA * (t + 1))
                at_least(pool, z_stored, DMA * t)
                nc.gpsimd.tensor_tensor(out=z_out[:], in0=y_n[:], in1=x_res[:], op=ALU.add).then_inc(z_ready, 1)

            def attend(n, q, tile=None, wo=False):
                for i in range(TT // 2, TT):
                    finish_o(n - 1, q - 1, 1, i)
                make_bias(n, q, 1)
                for i in range(TT):
                    finish_o(n, q, 0, i)
                    if wo and i in (1, 2):
                        split_wo(n - 1, i - 1)
                    if i == 0 and tile is not None and not (isinstance(tile, int) and tile == 0):
                        add_residual(tile - 1)
                make_bias(n + 1, q + 1, 0)
                for i in range(TT // 2):
                    finish_o(n, q, 1, i)
                    if wo:
                        split_wo(n - 1, TT // 2 + i)
                if tile is not None:
                    inverse_root(1, y_var, tile + 1, y_rstd)

            pool.wait_ge(gemm_done, NGEMM * (B - 1) + QC + KVC)
            make_bias(0, 0, 0)
            make_bias(0, 0, 1)
            pool.wait_ge(vn_loaded, 2 * DMA)
            for i in range(TT):
                finish_o(0, 0, 0, i)
            make_bias(1, 1, 0)
            for i in range(TT // 2):
                finish_o(0, 0, 1, i)
            with pool.Fori(1, LAG) as n:
                attend(n, n, wo=True)
            attend(LAG, 1, 0)
            with pool.Fori(1, TT) as i:
                attend(LAG + i, i + 1, i)
            with pool.Fori(0, TT) as i:
                attend(LAG + TT + i, i + 1, TT + i)
            with pool.Fori(0, TT - 1) as i:
                attend(LAG + 2 * TT + i, i + 1, 2 * TT + i)
            for i in range(TT // 2, TT):
                finish_o(B * TT - 1, TT - 1, 1, i)
            add_residual(B * TT - LAG - 1)
            inverse_root(TT, z_var, 1, z_rstd)
            with pool.Fori(B * TT - LAG, B * TT) as t:
                inverse_root(1, y_var, t + 1, y_rstd)
                add_residual(t)

            pool.wait_ge(lo_counted, 1)
            nc.gpsimd.tensor_reduce(lo_total[:], lo_count[:], mybir.AxisListType.C, ALU.add).then_inc(lo_summed, 1)

            def feed_forward(m, last=False):
                if not last:
                    inverse_root(TT, z_var, m + 2, z_rstd)
                inverse_root(TT, f_var, m + 1, f_rstd)
                pool.wait_ge(res_loaded, DMA * (m + 1))
                for i in range(TT):
                    pool.wait_ge(f_normed, TT * m + i + 1)
                    nc.gpsimd.tensor_tensor(out=y_s[:, i], in0=y_s[:, i], in1=z_res[:, i], op=ALU.add).then_inc(f_sum, 1)

            with pool.Fori(0, B - 1) as m:
                feed_forward(m)
            feed_forward(B - 1, last=True)

        @block.scalar
        def _(act):
            act.wait_ge(const_ready, CONSTANTS)
            nc.scalar.activation(warm[:], ones[:, 0:1], ACT.Sqrt)

            def round_xT(b):
                at_least(act, gemm_done, NGEMM * b)
                for kc in range(KC):
                    act.wait_ge(xT_psum, KC * b + kc + 1)
                    nc.scalar.activation(xT_hi[:, kc], bank[4 + kc][:], ACT.Copy).then_inc(xT_hi_ready, 1)

            def norm(b, f):
                if f:
                    round_raw(b, f - 1)
                if f == QC + KVC - 1:
                    round_raw(b, f)

            def round_weights(j):
                act.wait_ge(w_loaded[j % 2], DMA * (j // 2 + 1))
                if j == WBLOCKS - 1:
                    act.wait_ge(v_scaled, 1)
                nc.scalar.activation(w_hi[:, j], w_stage[:, j % 2], ACT.Copy).then_inc(w_hi_ready, 1)

            def square_v():
                act.wait_ge(w_loaded[1], DMA * WBLOCKS // 2)
                for kc in range(KC):
                    nc.scalar.activation(raw[:, QC + kc], w_stage[:, 1, kc], ACT.Square).then_inc(v_squared, 1)

            def norm_of_v():
                act.wait_ge(v_norm_psum, 1)
                nc.scalar.activation(raw[:, QC + KVC - 1], bank[7][:], ACT.Sqrt, scale=VSCALE ** -2,
                                     bias=eps_tiny[:]).then_inc(v_norm_ready, 1)

            def round_raw(b, f):
                act.wait_ge(scaled, (QC + KVC) * b + f + 1)
                at_least(act, qk_stored[f % QK_RING], qk_stores(b, f))
                nc.scalar.activation(qk[:, f % QK_RING, 0], raw[:, f], ACT.Copy).then_inc(qk_hi_ready, 1)

            def project(b, last=False):
                first = isinstance(b, int) and b == 0
                for kind, n in SCHEDULE:
                    if kind == "norm":
                        norm(b, n)
                    elif kind == "late norm":
                        if not first:
                            norm(b - 1, n)
                    elif kind == "root":
                        act.wait_ge(ssq_psum, 2 * b + n + 1)
                        if first and n == 1:
                            act.wait_ge(v_scaled, 1)
                        nc.scalar.activation(inv_rms[:, n], bank[6 + n][:], ACT.Sqrt, scale=1.0 / (D if n else H * HD),
                                             bias=eps_rms[:]).then_inc(root_ready, 1)
                    elif kind == "gemm" and n < QC + KVC:
                        if first and n in WEIGHTS_DUE:
                            round_weights(WEIGHTS_DUE.index(n) + 1)
                        if first and n == QC - 1:
                            square_v()
                        if first and n == QC:
                            norm_of_v()
                        if first and n == QC + KVC - 1:
                            act.wait_ge(vn_stored, DMA)
                            act.wait_ge(v_inv_ready, 1)
                        act.wait_ge(gemm_done, NGEMM * b + n + 1)
                        at_least(act, qk_ready, (QC + KVC) * (b - 1) + n + 1)
                        nc.scalar.activation(raw[:, n], bank[n % 4][:], ACT.Copy).then_inc(raw_ready, 1)
                        if n in (0, QC):
                            at_least(act, ssq_psum, 2 * (b - 1) + n // QC + 1)
                            dst = sum_sq[:, n // QC]
                        else:
                            m = n - 1 - n // QC
                            at_least(act, acc_ready, NSQ * b + m - 1)
                            dst = square[:, m % 2]
                        nc.scalar.activation(dst, bank[n % 4][:], ACT.Square).then_inc(sq_ready, 1)
                    elif kind == "gemm":
                        i = n - QC - KVC
                        if n == NGEMM - 1 and not last:
                            round_xT(b + 1)
                        act.wait_ge(gemm_done, NGEMM * b + n + 1)
                        at_least(act, v_stored, DMA * b)
                        nc.scalar.activation(v_out[:, :, i, 0], bank[n % 4][:].rearrange("p (g d) -> p g d", g=G),
                                             ACT.Copy).then_inc(v_hi_ready, 1)

            round_weights(0)
            round_xT(0)
            project(0)
            with act.Fori(1, B - 1) as b:
                project(b)
            project(B - 1, last=True)

            nc.scalar.activation(warm[:], ones[:, 0:1], ACT.Exp)

            def exps(n, u):
                A, i, r = UNITS * n + u, u // REP % TT, u % REP
                a, w = 2 * TT * n + u // REP, P * window(i)[1]
                act.wait_ge(u_ready, A + 1)
                at_least(act, pT_psum, A - RING + 1)
                if r == 0:
                    at_least(act, inv_sum_ready, a - TT + 1)
                nc.scalar.activation(p_sb[:, u % RING, 0:w], u_sb[:, u % RING, 0:w], ACT.Exp, scale=-1.0,
                                     bias=low[:, u % RING:u % RING + 1],
                                     accum_out=p_sum[:, i, r:r + 1]).then_inc(p_ready, 1)

            def round_pT(n, u):
                A, w = UNITS * n + u, P * window(u // REP % TT)[1]
                act.wait_ge(pT_psum, A + 1)
                at_least(act, pv_done, A - RING + 1)
                nc.scalar.activation(pT_hi[:, u % RING, 0:w], bank[2 + u % 2][:, 0:w], ACT.Copy).then_inc(pT_hi_ready, 1)

            def copy_low(n, u):
                act.wait_ge(pv_done, UNITS * n + u + 1)
                at_least(act, o_raw_ready, 2 * TT * n + u // REP)
                nc.scalar.activation(o_low[:], bank[4 + u // REP % 2][:].rearrange("p (r t d) -> p r t d", r=REP, t=2)[:, :, 1],
                                     ACT.Copy).then_inc(o_low_ready, 1)

            def round_oT(t, m, banks=(6,)):
                act.wait_ge(oT_psum, 4 * t + m + 1)
                at_least(act, oT_used, 4 * t + m - 1)
                nc.scalar.activation(oT_hi[:, m % 2].rearrange("p c n -> p (c n)"), bank[banks[m % len(banks)]][:], ACT.Copy).then_inc(oT_hi_ready, 1)

            def unit_work(n, u):
                for stage, nn, uu in due(n, u):
                    work = {"transpose": round_pT, "exps": exps, "copy_low": copy_low}.get(stage)
                    if work:
                        work(nn, uu)

            def attend(n, tile=None):
                for u in range(UNITS):
                    unit_work(n, u)
                    if isinstance(n, int) and n == 0 and u + LATE < QC + KVC:
                        norm(B - 1, u + LATE)
                    m, at = divmod(u - START - 1, STEP)
                    if tile is not None and m in range(4) and at == 0:
                        round_oT(tile, m)

            attention_loops(act, attend)
            for u in range(UNITS, UNITS + DRAIN):
                unit_work(B * TT - 1, u)

            def finish_tile(t):
                for m in range(4):
                    round_oT(t, m, TAIL_BANKS)

            def round_zT(m):
                for kc in range(KC):
                    act.wait_ge(zT_psum, KC * m + kc + 1)
                    nc.scalar.activation(zT_hi[:, kc], bank[kc][:], ACT.Copy).then_inc(zT_hi_ready, 1)

            def round_piece(j):
                src, hi, _ = piece(j)
                act.wait_ge(f_loaded[j % 2], DMA * (j // 2 + 1))
                nc.scalar.activation(hi, src, ACT.Copy).then_inc(f_hi_ready, 1)

            for k in range(LAG):
                finish_tile(B * TT - LAG + k)
                if k == 0:
                    round_zT(0)
                if k in (1, 2):
                    round_piece(k - 1)
            round_piece(2)

            nc.scalar.activation(warm[:], ones[:, 0:1], ACT.Silu)
            act.wait_ge(scales_loaded, 3 * DMA)

            def feed_forward(m, last=False):
                for c in range(IC):
                    C = IC * m + c
                    act.wait_ge(gu_psum, 2 * C + 1)
                    at_least(act, hid_ready, C)
                    nc.scalar.activation(silu[:], bank[2 * (c % 2)][:], ACT.Silu, scale=gate_sc[:, c:c + 1]).then_inc(silu_ready, 1)
                    act.wait_ge(hid_ready, C + 1)
                    at_least(act, down_done, C - 1 + (c == 0))
                    nc.scalar.activation(h_hi[:, c % 2], hid[:], ACT.Copy).then_inc(h_hi_ready, 1)
                    if isinstance(m, int) and m == 0 and c + 3 < len(PIECES):
                        if c == 0:
                            act.wait_ge(z_stored, DMA * B * TT)
                        round_piece(c + 3)
                if not last:
                    round_zT(m + 1)

            feed_forward(0)
            with act.Fori(1, B - 1) as m:
                feed_forward(m)
            feed_forward(B - 1, last=True)

        @block.vector
        def _(dve):
            def layer_stats(k, loaded, value, tiles, stats_ready, moments_ready, var_ready):
                count = len(tiles)
                dve.wait_ge(loaded, value)
                for i, tile in enumerate(tiles):
                    nc.vector.bn_stats(stats[:, i], tile).then_inc(stats_ready, 1)
                for i in range(count):
                    dve.wait_ge(stats_ready, count * k + i + 1)
                    hold(dve)
                    nc.vector.bn_aggr(moments[:, i], stats[:, i]).then_inc(moments_ready, 1)
                dve.wait_ge(moments_ready, count * k + count)
                nc.vector.tensor_scalar_add(var_eps[:, 0:count], moments[:, 0:count, 1], LN_EPS).then_inc(var_ready, 1)

            def layer_norm(k, dst, src, i, rstd_ready, normed):
                dve.wait_ge(rstd_ready, k + 1)
                nc.vector.tensor_scalar(dst, src, moments[:, i, 0:1], rstd[:, i:i + 1], ALU.subtract, ALU.mult).then_inc(normed, 1)

            def stats_x(b):
                layer_stats(b, x_loaded, DMA * (b + 1), [x_in[:, i] for i in range(TT)], ln_stats, ln_moments, ln_var)

            def norm_x(b):
                for i in range(TT):
                    layer_norm(b, x_in[:, i], x_in[:, i], i, ln_rstd, ln_done)

            def split_xT(b):
                for kc in range(KC):
                    dve.wait_ge(xT_hi_ready, KC * b + kc + 1)
                    nc.vector.tensor_tensor(xT_lo[:, kc], bank[4 + kc][:], xT_hi[:, kc].bitcast(F32), ALU.subtract).then_inc(xT_ready, 1)

            def split_weights(j):
                dve.wait_ge(w_hi_ready, j + 1)
                nc.vector.tensor_tensor(w_lo[:, j], w_stage[:, j % 2], w_hi[:, j].bitcast(F32), ALU.subtract).then_inc(w_ready, 1)

            def scale_v():
                dve.wait_ge(w_loaded[1], DMA * WBLOCKS // 2)
                dve.wait_ge(v_norm_ready, 1)
                nc.vector.reciprocal(inv_rms[:, 1], raw[:, QC + KVC - 1]).then_inc(v_inv_ready, 1)
                dve.wait_ge(v_inv_ready, 1)
                nc.vector.tensor_tensor(w_stage[:, 1], w_stage[:, 1], inv_rms[:, 1:2].broadcast_to([P, KC, T]), ALU.mult).then_inc(v_scaled, 1)

            def split_raw(b, f):
                dve.wait_ge(qk_hi_ready, (QC + KVC) * b + f + 1)
                nc.vector.tensor_tensor(qk[:, f % QK_RING, 1], raw[:, f], qk[:, f % QK_RING, 0].bitcast(F32), ALU.subtract).then_inc(qk_ready, 1)

            def norm(b, f):
                dve.wait_ge(inv_ready, 2 * b + f // QC + 1)
                nc.vector.scalar_tensor_tensor(raw[:, f], raw[:, f], norm_w[:, f:f + 1], inv_rms[:, f // QC],
                                               ALU.mult, ALU.mult).then_inc(scaled, 1)
                if f:
                    split_raw(b, f - 1)
                if f == QC + KVC - 1:
                    split_raw(b, f)

            def project(b, last=False):
                first = isinstance(b, int) and b == 0
                for kind, n in SCHEDULE:
                    if kind == "norm":
                        norm(b, n)
                    elif kind == "late norm":
                        if not first:
                            norm(b - 1, n)
                    elif kind == "root":
                        dve.wait_ge(root_ready, 2 * b + n + 1)
                        nc.vector.reciprocal(inv_rms[:, n], inv_rms[:, n]).then_inc(inv_ready, 1)
                    elif n < QC + KVC:
                        if first and n == QC + 1:
                            scale_v()
                        if first and n in WEIGHTS_DUE:
                            split_weights(WEIGHTS_DUE.index(n) + 1)
                        if not last and n == QC - 4:
                            stats_x(b + 1)
                        if n not in (0, QC):
                            m = n - 1 - n // QC
                            dve.wait_ge(sq_ready, (QC + KVC) * b + n + 1)
                            at_least(dve, acc_ready, NSQ * b + m)
                            nc.vector.tensor_tensor(sum_sq[:, n // QC], sum_sq[:, n // QC], square[:, m % 2], ALU.add).then_inc(acc_ready, 1)
                    else:
                        if n == QC + KVC and not last:
                            norm_x(b + 1)
                        if n == NGEMM - 1 and not last:
                            split_xT(b + 1)
                        dve.wait_ge(v_hi_ready, TT * b + n - QC - KVC + 1)
                        i = n - QC - KVC
                        nc.vector.tensor_tensor(v_out[:, :, i, 1], bank[n % 4][:].rearrange("p (g d) -> p g d", g=G), v_out[:, :, i, 0],
                                                ALU.subtract).then_inc(v_ready, 1)

            stats_x(0)
            split_weights(0)
            norm_x(0)
            dve.wait_ge(norm_loaded, 2 * DMA)
            nc.vector.tensor_scalar_mul(norm_w[:, 0:QC], qn_raw[:], -HD ** -0.5).then_inc(norm_ready, 1)
            split_xT(0)
            dve.wait_ge(norm_ready, 1)
            project(0)
            with dve.Fori(1, B - 1) as b:
                project(b)
            project(B - 1, last=True)

            def add_bias(n, u):
                A, i = UNITS * n + u, u // REP % TT
                _, tiles, at = window(i)
                w = P * tiles
                if u % (UNITS // 2) == 0:
                    dve.wait_ge(bias_ready, 2 * n + 2 * u // UNITS + 1)
                dve.wait_ge(s_psum, A + 1)
                at_least(dve, p_ready, A - RING + 1)
                hold(dve)
                nc.vector.tensor_tensor_reduce(out=u_sb[:, u % RING, 0:w], in0=bank[u % 2][:, 0:w],
                                               in1=bias[:, 2 * u // UNITS, u % REP, at:at + w], scale=1.0, scalar=BIG,
                                               op0=ALU.add, op1=ALU.min, accum_out=low[:, u % RING:u % RING + 1]).then_inc(u_ready, 1)

            def split_pT(n, u):
                w = P * window(u // REP % TT)[1]
                dve.wait_ge(pT_hi_ready, UNITS * n + u + 1)
                nc.vector.tensor_tensor(pT_lo[:, u % RING, 0:w], bank[2 + u % 2][:, 0:w], pT_hi[:, u % RING, 0:w],
                                        ALU.subtract).then_inc(pT_ready, 1)

            def invert_sums(n, u):
                a = 2 * TT * n + u // REP
                dve.wait_ge(p_ready, UNITS * n + u + 1)
                at_least(dve, o_mid_ready, a - 1)
                nc.vector.reciprocal(inv_sum[:, u // REP % 2], p_sum[:, u // REP % TT]).then_inc(inv_sum_ready, 1)

            def add_low(n, u):
                a = 2 * TT * n + u // REP
                dve.wait_ge(o_low_ready, a + 1)
                at_least(dve, o_mid_ready, a - 1)
                nc.vector.tensor_tensor(o_raw[:, u // REP % 2],
                                        bank[4 + u // REP % 2][:].rearrange("p (r t d) -> p r t d", r=REP, t=2)[:, :, 0],
                                        o_low[:], ALU.add).then_inc(o_raw_ready, 1)

            def split_oT(t, m, banks=(6,)):
                dve.wait_ge(oT_hi_ready, 4 * t + m + 1)
                nc.vector.tensor_tensor(oT_lo[:, m % 2].rearrange("p c n -> p (c n)"), bank[banks[m % len(banks)]][:],
                                        oT_hi[:, m % 2].rearrange("p c n -> p (c n)").bitcast(F32), ALU.subtract).then_inc(oT_ready, 1)

            def stats_y(t, acc):
                layer_stats(t, oT_used, 4 * t + 4, [acc[:]], y_stats, y_moments, y_var)

            def norm_y(t, acc):
                at_least(dve, z_ready, t)
                layer_norm(t, y_n[:], acc[:], 0, y_rstd, y_normed)

            def unit_work(n, u):
                for stage, nn, uu in due(n, u):
                    work = {"scores": add_bias, "split": split_pT, "invert_sums": invert_sums, "add_low": add_low}.get(stage)
                    if work:
                        work(nn, uu)

            def attend(n, tile=None):
                for u in range(UNITS):
                    unit_work(n, u)
                    if isinstance(n, int) and n == 0 and u + LATE < QC + KVC:
                        norm(B - 1, u + LATE)
                    m, at = divmod(u - START - 2, STEP)
                    if tile is not None and m in range(4) and at == 0:
                        split_oT(tile, m)
                    if u == START and tile is not None and not (isinstance(tile, int) and tile == 0):
                        norm_y(tile - 1, bank[7])
                if tile is not None:
                    stats_y(tile, bank[7])

            attention_loops(dve, attend)
            for u in range(UNITS, UNITS + DRAIN):
                unit_work(B * TT - 1, u)

            def stats_z(m):
                layer_stats(m, z_loaded, DMA * (m + 1), [z_in[:, i] for i in range(TT)], z_stats, z_moments, z_var)

            def norm_z(m):
                for i in range(TT):
                    layer_norm(m, z_in[:, i], z_in[:, i], i, z_rstd, z_normed)

            def split_zT(m):
                for kc in range(KC):
                    dve.wait_ge(zT_hi_ready, KC * m + kc + 1)
                    nc.vector.tensor_tensor(zT_lo[:, kc], bank[kc][:], zT_hi[:, kc].bitcast(F32), ALU.subtract).then_inc(zT_ready, 1)

            def split_piece(j):
                src, hi, lo = piece(j)
                dve.wait_ge(f_hi_ready, j + 1)
                nc.vector.tensor_tensor(lo, src, hi.bitcast(F32), ALU.subtract).then_inc(lo_ready, 1)
                dve.wait_ge(lo_ready, j + 1)
                nc.vector.tensor_scalar(src, lo.bitcast(F32), 0.0, 0.0, ALU.not_equal, ALU.add,
                                        accum_out=lo_counts[:, j:j + 1]).then_inc(f_ready, 1)
                if j == len(PIECES) - 1:
                    dve.wait_ge(f_ready, j + 1)
                    nc.vector.tensor_reduce(lo_count[:], lo_counts[:], mybir.AxisListType.X, ALU.add).then_inc(lo_counted, 1)

            def finish_tile(k):
                t, acc, acc_before = B * TT - LAG + k, bank[5 + 2 * (k % 2)], bank[7 - 2 * (k % 2)]
                for m in range(4):
                    split_oT(t, m, TAIL_BANKS)
                    if m == 0:
                        norm_y(t - 1, acc_before)
                    if m == 2 and k == 0:
                        stats_z(0)
                        norm_z(0)
                if k in (1, 2):
                    split_piece(k - 1)
                stats_y(t, acc)

            for k in range(LAG):
                finish_tile(k)
                if k == 0:
                    split_zT(0)
            norm_y(B * TT - 1, bank[5])

            split_piece(2)

            def feed_forward(m, last=False):
                first = isinstance(m, int) and m == 0
                for c in range(IC):
                    C = IC * m + c
                    if not last and c == IC - 2:
                        stats_z(m + 1)
                    if not last and c == IC - 1:
                        norm_z(m + 1)
                    dve.wait_ge(gu_psum, 2 * C + 2)
                    dve.wait_ge(silu_ready, C + 1)
                    at_least(dve, h_ready, C)
                    nc.vector.scalar_tensor_tensor(hid[:], bank[2 * (c % 2) + 1][:], up_sc[:, c:c + 1], silu[:],
                                                   ALU.mult, ALU.mult).then_inc(hid_ready, 1)
                    dve.wait_ge(h_hi_ready, C + 1)
                    nc.vector.tensor_tensor(h_lo[:, c % 2], hid[:], h_hi[:, c % 2].bitcast(F32), ALU.subtract).then_inc(h_ready, 1)
                    if first and c + 3 < len(PIECES):
                        split_piece(c + 3)
                if not last:
                    split_zT(m + 1)
                dve.wait_ge(down_done, IC * (m + 1))
                at_least(dve, out_stored, DMA * m)
                for i in range(TT):
                    nc.vector.tensor_tensor(y_s[:, i], bank[4 + i][:], down_sc[:], ALU.mult).then_inc(ys_ready, 1)
                layer_stats(m, ys_ready, TT * (m + 1), [y_s[:, i] for i in range(TT)], f_stats, f_moments, f_var)
                for i in range(TT):
                    layer_norm(m, y_s[:, i], y_s[:, i], i, f_rstd, f_normed)

            dve.wait_ge(scales_loaded, 3 * DMA)
            feed_forward(0)
            with dve.Fori(1, B - 1) as m:
                feed_forward(m)
            feed_forward(B - 1, last=True)

        @block.tensor
        def _(pe):
            pe.wait_ge(const_ready, CONSTANTS)

            def transpose_x(b):
                pe.wait_ge(ln_done, TT * b + TT)
                at_least(pe, root_ready, 2 * b)
                for kc in range(KC):
                    for i in range(TT):
                        last = nc.tensor.transpose(bank[4 + kc][:, P * i:P * i + P], x_in[:, i, P * kc:P * kc + P], ident[:])
                    last.then_inc(xT_psum, 1)

            def sum_squares(b, n):
                pe.wait_ge(acc_ready, NSQ * b + (NSQ if n else QC - 1))
                pe.wait_ge(sq_ready, (QC + KVC) * b + (QC + KVC if n else QC))
                at_least(pe, root_ready, 2 * (b - 1) + n + 1)
                if n and isinstance(b, int) and b == 0:
                    pe.wait_ge(v_norm_ready, 1)
                nc.tensor.matmul(bank[6 + n][:], ones[:], sum_sq[:, n], start=True, stop=True).then_inc(ssq_psum, 1)

            def project(b, last=False):
                first = isinstance(b, int) and b == 0
                for n in range(NGEMM):
                    if first and n == QC:
                        for kc in range(KC):
                            pe.wait_ge(v_squared, kc + 1)
                            mm = nc.tensor.matmul(bank[7][:], ones[:], raw[:, QC + kc], start=(kc == 0), stop=(kc == KC - 1))
                        mm.then_inc(v_norm_psum, 1)
                    if first and n % 4 == 0:
                        pe.wait_ge(w_ready, n // 4 + 1)
                    if n < 4:
                        at_least(pe, v_ready, TT * (b - 1) + n + 1)
                    else:
                        pe.wait_ge(sq_ready, (QC + KVC) * b + n - 4 + 1)
                    if n == NGEMM - 1 and not last:
                        transpose_x(b + 1)
                    for kc in range(KC):
                        if n == 0:
                            pe.wait_ge(xT_ready, KC * b + kc + 1)
                        if n < QC + KVC:
                            j, cols = n // TT, slice(P * (n % TT), P * (n % TT) + P)
                            parts = part_products(w_hi[:, j, kc, cols], w_lo[:, j, kc, cols], xT_hi[:, kc], xT_lo[:, kc])
                        else:
                            i = n - QC - KVC
                            tokens = slice(P * i, P * i + P)
                            parts = part_products(xT_hi[:, kc, tokens], xT_lo[:, kc, tokens], w_hi[:, WBLOCKS - 1, kc], w_lo[:, WBLOCKS - 1, kc])
                        for k, (lhs, rhs) in enumerate(parts):
                            mm = nc.tensor.matmul(bank[n % 4][:], lhs, rhs, start=(kc == 0 and k == 0), stop=(kc == KC - 1 and k == 2))
                    mm.then_inc(gemm_done, 1)
                    if n == QC + 1:
                        sum_squares(b, 0)
                    if n == QC + KVC:
                        sum_squares(b, 1)

            transpose_x(0)
            project(0)
            with pe.Fori(1, B - 1) as b:
                project(b)
            project(B - 1, last=True)

            def scores(n, u):
                A, s, i, r = UNITS * n + u, 2 * u // UNITS, u // REP % TT, u % REP
                key, tiles, _ = window(i)
                w = P * tiles
                if u % (UNITS // 2) == 0:
                    pe.wait_ge(heads_loaded[s], 4 * DMA * (n + 1))
                at_least(pe, u_ready, A - 1)
                for part in range(2):
                    mm = nc.tensor.matmul(bank[u % 2][:, 0:w], q_st[:, s, r, P * i:P * i + P],
                                          k_st[:, s, part, P * key:P * key + w], start=(part == 0), stop=(part == 1))
                mm.then_inc(s_psum, 1)

            def transpose_p(n, u):
                A, tiles = UNITS * n + u, window(u // REP % TT)[1]
                pe.wait_ge(p_ready, A + 1)
                at_least(pe, pT_ready, A - 1)
                for j in range(tiles):
                    mm = nc.tensor.transpose(bank[2 + u % 2][:, P * j:P * j + P], p_sb[:, u % RING, P * j:P * j + P], ident[:])
                mm.then_inc(pT_psum, 1)

            def weigh_values(n, u):
                A, s, r, ring = UNITS * n + u, 2 * u // UNITS, u % REP, u % RING
                key, tiles, _ = window(u // REP % TT)
                acc = bank[4 + u // REP % 2][:, 2 * HD * r:2 * HD * r + 2 * HD]
                pe.wait_ge(pT_ready, A + 1)
                if r == 0:
                    at_least(pe, o_raw_ready, 2 * TT * n + u // REP - 1)
                for j in range(tiles):
                    nc.tensor.matmul(acc, pT_hi[:, ring, P * j:P * j + P], v_st[:, s, key + j],
                                     start=(j == 0), stop=False, skip_group_check=True)
                    mm = nc.tensor.matmul(acc[:, 0:HD], pT_lo[:, ring, P * j:P * j + P], v_st[:, s, key + j, 0:HD],
                                          start=False, stop=(j == tiles - 1), skip_group_check=True)
                mm.then_inc(pv_done, 1)

            def transpose_o(t, m, banks=(6,)):
                if m == 0:
                    pe.wait_ge(tile_loaded, DMA * (t + 1))
                at_least(pe, oT_ready, 4 * t + m + 1 - len(banks))
                for c in range(4):
                    mm = nc.tensor.transpose(bank[banks[m % len(banks)]][:, P * c:P * c + P], o_in[:, m, P * c:P * c + P], ident[:])
                mm.then_inc(oT_psum, 1)

            def project_o(t, m, products, acc):
                for j in products:
                    if j == 0:
                        pe.wait_ge(oT_ready, 4 * t + m + 1)
                    c, k = divmod(j, 3)
                    chunk = 4 * m + c
                    lhs, rhs = part_products(oT_hi[:, m % 2, c], oT_lo[:, m % 2, c], wo_hi[:, chunk], wo_lo[:, chunk])[k]
                    mm = nc.tensor.matmul(acc[:], lhs, rhs, start=(chunk == 0 and k == 0), stop=(chunk == QC - 1 and k == 2))
                    if j == 11:
                        mm.then_inc(oT_used, 1)

            def unit_work(n, u):
                for stage, nn, uu in due(n, u):
                    work = {"scores": scores, "transpose": transpose_p, "weigh": weigh_values}.get(stage)
                    if work:
                        work(nn, uu)

            def attend(n, tile=None):
                for u in range(UNITS):
                    unit_work(n, u)
                    if tile is not None:
                        m, at = divmod(u - START, STEP)
                        if m in range(4) and at == 0:
                            transpose_o(tile, m)
                        m, at = divmod(u - START - 4, STEP)
                        if m in range(4):
                            if m == 0 and at == 0:
                                at_least(pe, y_normed, tile)
                                if isinstance(tile, int):
                                    pe.wait_ge(wo_ready, QC)
                            project_o(tile, m, (2 * at, 2 * at + 1), bank[7])

            pe.wait_ge(v_ready, TT * B)
            attention_loops(pe, attend)
            for u in range(UNITS, UNITS + DRAIN):
                unit_work(B * TT - 1, u)

            def finish_tile(t, acc):
                transpose_o(t, 0, TAIL_BANKS)
                at_least(pe, y_normed, t - 1)
                for m in range(4):
                    if m < 3:
                        transpose_o(t, m + 1, TAIL_BANKS)
                    project_o(t, m, range(12), acc)

            pe.wait_ge(o_raw_ready, 2 * TT * B * TT)
            def transpose_z(m):
                pe.wait_ge(z_normed, TT * m + TT)
                for kc in range(KC):
                    at_least(pe, hid_ready, IC * m if kc < 2 else IC * m - 1)
                    for i in range(TT):
                        mm = nc.tensor.transpose(bank[kc][:, P * i:P * i + P], z_in[:, i, P * kc:P * kc + P], ident[:])
                    mm.then_inc(zT_psum, 1)

            finish_tile(B * TT - LAG, bank[5])
            transpose_z(0)
            with pe.Fori(0, TT // 2) as i:
                finish_tile(B * TT - TT + 2 * i, bank[7])
                finish_tile(B * TT - TT + 1 + 2 * i, bank[5])

            def products(lhs, rhs, exact):
                return [p for k, p in enumerate(part_products(*lhs, *rhs)) if k != {"lhs": 1, "rhs": 2}.get(exact)]

            def accumulate(acc, products, first, last):
                for k, (lhs, rhs) in enumerate(products):
                    mm = nc.tensor.matmul(acc, lhs, rhs, start=(first and k == 0), stop=(last and k == len(products) - 1))
                return mm

            def gate_and_up(m, c, exact):
                C = IC * m + c
                for g in range(2):
                    if c:
                        at_least(pe, hid_ready, C - 1)
                    for kc in range(KC):
                        if c == 0 and g == 0:
                            pe.wait_ge(zT_ready, KC * m + KC)
                        w = [gu[c // PIECE][:, part, kc, g, P * (c % PIECE):P * (c % PIECE) + P] for part in range(2)]
                        mm = accumulate(bank[2 * (c % 2) + g][:], products(w, (zT_hi[:, kc], zT_lo[:, kc]), "lhs" if exact else None),
                                        kc == 0, kc == KC - 1)
                    mm.then_inc(gu_psum, 1)

            def down(m, c, exact):
                if isinstance(m, int) and m == 0 and c % PIECE == 0:
                    pe.wait_ge(f_ready, c + 3)
                    if c == 0:
                        pe.wait_ge(y_normed, B * TT)
                pe.wait_ge(h_ready, IC * m + c + 1)
                for i in range(TT):
                    if c == 0:
                        at_least(pe, ys_ready, TT * (m - 1) + i + 1)
                    h = [x[:, c % 2, P * i:P * i + P] for x in (h_hi, h_lo)]
                    w = [dn[c // PIECE][:, part, c % PIECE] for part in range(2)]
                    mm = accumulate(bank[4 + i][:], products(h, w, "rhs" if exact else None), c == 0, c == IC - 1)
                mm.then_inc(down_done, 1)

            def feed_forward(m, last=False, exact=False):
                for c in range(IC):
                    if isinstance(m, int) and m == 0 and c % PIECE == 0:
                        pe.wait_ge(f_ready, c + 2)
                    gate_and_up(m, c, exact)
                    if c:
                        down(m, c - 1, exact)
                if not last:
                    transpose_z(m + 1)
                down(m, IC - 1, exact)

            feed_forward(0)
            pe.wait_ge(lo_summed, 1)
            hold(pe)
            lo_used = pe.value_load(lo_total[:].bitcast(mybir.dt.int32))

            def feed_forward_either(m, last=False):
                with pe.If(lo_used == 0):
                    feed_forward(m, last, exact=True)
                with pe.Else():
                    feed_forward(m, last)
                hold(pe)

            with pe.Fori(1, B - 1) as m:
                feed_forward_either(m)
            feed_forward_either(B - 1, last=True)


def kernel(L0_attn_x, L0_attn_wq, L0_attn_wk, L0_attn_wv, L0_attn_wo, L0_attn_q_norm_w, L0_attn_k_norm_w,
           L0_ffn_gate_w, L0_ffn_up_w, L0_ffn_down_w, L0_ffn_gate_s, L0_ffn_up_s, L0_ffn_down_s):
    import concourse.bacc as bacc
    from concourse.bass_utils import run_bass_kernel_spmd

    def columns(a):
        return a.reshape(-1, P).T

    arrays = {
        "x": L0_attn_x, "wqT": np.transpose(L0_attn_wq), "wkT": np.transpose(L0_attn_wk),
        "wvT": np.transpose(L0_attn_wv), "woT": np.transpose(L0_attn_wo), "q_norm": columns(L0_attn_q_norm_w),
        "k_norm": columns(L0_attn_k_norm_w), "gateT": np.transpose(L0_ffn_gate_w), "upT": np.transpose(L0_ffn_up_w),
        "downT": np.transpose(L0_ffn_down_w), "gate_s": columns(L0_ffn_gate_s), "up_s": columns(L0_ffn_up_s), "down_s": L0_ffn_down_s,
    }
    arrays = {name: np.ascontiguousarray(a) for name, a in arrays.items()}
    nc = bacc.Bacc("TRN2", target_bir_lowering=False, num_devices=1)
    args = {name: nc.dram_tensor(name, a.shape, mybir.dt.from_np(a.dtype), kind="ExternalInput").ap() for name, a in arrays.items()}
    out = nc.dram_tensor("out", (B, T, D), F32, kind="ExternalOutput").ap()
    sandwich_layer(nc, **args, out=out)
    result = run_bass_kernel_spmd(nc, [arrays], core_ids=[0])
    return result.results[0]["out"]
```
